# Optimizing a Trainium2 kernel written in Bass

```python
import numpy as np
import jax
import jax.numpy as jnp

def _softmax(x, axis=-1):
    return jax.nn.softmax(x, axis=axis)

def _gelu(x):
    return jax.nn.gelu(x, approximate=True)

def _silu(x):
    return jax.nn.silu(x)

def _sigmoid(x):
    return jax.nn.sigmoid(x)

def _layernorm(x, axis=-1, eps=1e-05):
    m = jnp.mean(x, axis=axis, keepdims=True)
    v = jnp.var(x, axis=axis, keepdims=True)
    return (x - m) / jnp.sqrt(v + eps)

def _scatter_add(tgt, idx, src, axis=0):
    return tgt.at[idx].add(src)

def _segment_sum(src, seg, n):
    return jax.ops.segment_sum(src, seg, n)
kernel_name = 'mk_adj_resnorm_d2_adj_r2_bbb956'

def setup_inputs(seed: int=0):
    np.random.seed(seed)
    _w = jnp.asarray

    def _rec_inputs():
        import jax
        import jax.numpy as jnp
        _gk = jax.random.key(seed)
        x = 7.22e-05 + 1 * jax.random.normal(jax.random.fold_in(_gk, 1), (64, 128, 256), jnp.float32)
        _w = (1.0 + jnp.arange(128, dtype=jnp.float32)) ** (-0.5)
        _w = _w / _w.mean()
        _pij = jnp.clip(0.125 * _w[:, None] * _w[None, :], 0.0, 1.0)
        _a = jax.random.uniform(jax.random.fold_in(_gk, 2), (128, 128)) < _pij
        adj = _a.astype(jnp.int32)
        return (x, adj)
    x, adj = _rec_inputs()

    def _L0_gnn_setup():
        import jax, jax.numpy as jnp
        import numpy as np
        LEAKY_ALPHA = 0.01
        NEG_INF = -1000000000.0
        LN_EPS = 1e-05

        def _gat_heads(x, adj, W, a):
            O = W.shape[-1]
            Wh = jnp.einsum('bnf,hfo->bhno', x, W)
            f1 = jnp.einsum('bhno,ho->bhn', Wh, a[:, :O])
            f2 = jnp.einsum('bhno,ho->bhn', Wh, a[:, O:])
            e = f1[:, :, :, None] + f2[:, :, None, :]
            e = jnp.where(e > 0, e, LEAKY_ALPHA * e)
            e = jnp.where(adj[None, None] > 0, e, NEG_INF)
            attn = jax.nn.softmax(e, axis=-1)
            return jnp.einsum('bhnm,bhmo->bhno', attn, Wh)
        key = jax.random.key(seed)
        ks = jax.random.split(key, 10)
        B, N, F_in, F_hid, H, F_out, D_ff = (8, 1024, 256, 256, 4, 256, 256)
        s = 0.05
        return {'enc_inputs': jax.random.normal(ks[0], (B, N, F_in), jnp.float32), 'adj': jax.random.randint(ks[1], (N, N), 0, 2, jnp.int32), 'W_heads': jax.random.normal(ks[2], (H, F_in, F_hid), jnp.float32) * s, 'a_heads': jax.random.normal(ks[3], (H, 2 * F_hid), jnp.float32) * s, 'W_out': jax.random.normal(ks[4], (H * F_hid, F_out), jnp.float32) * s, 'a_out': jax.random.normal(ks[5], (2 * F_out,), jnp.float32) * s, 'w1': jax.random.normal(ks[6], (F_out, D_ff), jnp.float32) * s, 'b1': jnp.zeros((D_ff,), jnp.float32), 'w2': jax.random.normal(ks[7], (D_ff, F_out), jnp.float32) * s, 'b2': jnp.zeros((F_out,), jnp.float32), 'ln_gamma': jnp.ones((F_out,), jnp.float32), 'ln_beta': jnp.zeros((F_out,), jnp.float32)}
    _L0_gnn_all = _L0_gnn_setup()
    _L0_gnn_in = {k: v for k, v in _L0_gnn_all.items() if k in ('W_heads', 'a_heads', 'W_out', 'a_out', 'w1', 'b1', 'w2', 'b2', 'ln_gamma', 'ln_beta')}
    del _L0_gnn_all

    def _L1_gnn_setup():
        import jax, jax.numpy as jnp
        import numpy as np
        D_MODEL = 256
        NUM_HEADS = 8
        D_HEAD = D_MODEL // NUM_HEADS
        B, N = (4, 1024)
        key = jax.random.key(seed)
        ks = jax.random.split(key, 10)
        s = 1.0 / np.sqrt(D_MODEL)
        inp = {'h': jax.random.normal(ks[0], (B, N, D_MODEL), dtype=jnp.float32), 'adj': jax.random.randint(ks[1], (N, N), 0, 2, dtype=jnp.int32), 'Wq': jax.random.uniform(ks[2], (D_MODEL, D_MODEL), jnp.float32, -s, s), 'bq': jax.random.uniform(ks[3], (D_MODEL,), jnp.float32, -s, s), 'Wk': jax.random.uniform(ks[4], (D_MODEL, D_MODEL), jnp.float32, -s, s), 'bk': jax.random.uniform(ks[5], (D_MODEL,), jnp.float32, -s, s), 'Wv': jax.random.uniform(ks[6], (D_MODEL, D_MODEL), jnp.float32, -s, s), 'bv': jax.random.uniform(ks[7], (D_MODEL,), jnp.float32, -s, s), 'Wo': jax.random.uniform(ks[8], (D_MODEL, D_MODEL), jnp.float32, -s, s), 'bo': jax.random.uniform(ks[9], (D_MODEL,), jnp.float32, -s, s)}
        return inp
    _L1_gnn_all = _L1_gnn_setup()
    _L1_gnn_in = {k: v for k, v in _L1_gnn_all.items() if k in ('Wq', 'bq', 'Wk', 'bk', 'Wv', 'bv', 'Wo', 'bo')}
    del _L1_gnn_all
    return {'x': x, 'adj': adj, 'L0_gnn_W_heads': _L0_gnn_in['W_heads'], 'L0_gnn_a_heads': _L0_gnn_in['a_heads'], 'L0_gnn_W_out': _L0_gnn_in['W_out'], 'L0_gnn_a_out': _L0_gnn_in['a_out'], 'L0_gnn_w1': _L0_gnn_in['w1'], 'L0_gnn_b1': _L0_gnn_in['b1'], 'L0_gnn_w2': _L0_gnn_in['w2'], 'L0_gnn_b2': _L0_gnn_in['b2'], 'L0_gnn_ln_gamma': _L0_gnn_in['ln_gamma'], 'L0_gnn_ln_beta': _L0_gnn_in['ln_beta'], 'L1_gnn_Wq': _L1_gnn_in['Wq'], 'L1_gnn_bq': _L1_gnn_in['bq'], 'L1_gnn_Wk': _L1_gnn_in['Wk'], 'L1_gnn_bk': _L1_gnn_in['bk'], 'L1_gnn_Wv': _L1_gnn_in['Wv'], 'L1_gnn_bv': _L1_gnn_in['bv'], 'L1_gnn_Wo': _L1_gnn_in['Wo'], 'L1_gnn_bo': _L1_gnn_in['bo']}

def reference(x, adj, L0_gnn_W_heads, L0_gnn_a_heads, L0_gnn_W_out, L0_gnn_a_out, L0_gnn_w1, L0_gnn_b1, L0_gnn_w2, L0_gnn_b2, L0_gnn_ln_gamma, L0_gnn_ln_beta, L1_gnn_Wq, L1_gnn_bq, L1_gnn_Wk, L1_gnn_bk, L1_gnn_Wv, L1_gnn_bv, L1_gnn_Wo, L1_gnn_bo):
    import jax
    import jax.numpy as jnp

    def _L0_gnn_ref(enc_inputs, adj, W_heads, a_heads, W_out, a_out, w1, b1, w2, b2, ln_gamma, ln_beta):
        import jax, jax.numpy as jnp
        import numpy as np
        LEAKY_ALPHA = 0.01
        NEG_INF = -1000000000.0
        LN_EPS = 1e-05

        def _gat_heads(x, adj, W, a):
            O = W.shape[-1]
            Wh = jnp.einsum('bnf,hfo->bhno', x, W)
            f1 = jnp.einsum('bhno,ho->bhn', Wh, a[:, :O])
            f2 = jnp.einsum('bhno,ho->bhn', Wh, a[:, O:])
            e = f1[:, :, :, None] + f2[:, :, None, :]
            e = jnp.where(e > 0, e, LEAKY_ALPHA * e)
            e = jnp.where(adj[None, None] > 0, e, NEG_INF)
            attn = jax.nn.softmax(e, axis=-1)
            return jnp.einsum('bhnm,bhmo->bhno', attn, Wh)
        B, N, _ = enc_inputs.shape
        h = jax.nn.elu(_gat_heads(enc_inputs, adj, W_heads, a_heads))
        h = jnp.transpose(h, (0, 2, 1, 3)).reshape(B, N, -1)
        out = _gat_heads(h, adj, W_out[None], a_out[None])[:, 0]
        out = jax.nn.elu(out)
        ffn = jnp.maximum(out @ w1 + b1, 0.0) @ w2 + b2
        y = ffn + out
        mu = jnp.mean(y, axis=-1, keepdims=True)
        var = jnp.var(y, axis=-1, keepdims=True)
        return (y - mu) / jnp.sqrt(var + LN_EPS) * ln_gamma + ln_beta

    def _L1_gnn_ref(h, adj, Wq, bq, Wk, bk, Wv, bv, Wo, bo):
        import jax, jax.numpy as jnp
        import numpy as np
        D_MODEL = 256
        NUM_HEADS = 8
        D_HEAD = D_MODEL // NUM_HEADS
        B, N = (4, 1024)
        b, n, _ = h.shape

        def split_heads(x):
            return x.reshape(b, n, NUM_HEADS, D_HEAD).transpose(0, 2, 1, 3)
        q = split_heads(h @ Wq.T + bq)
        k = split_heads(h @ Wk.T + bk)
        v = split_heads(h @ Wv.T + bv)
        scale = 1.0 / np.sqrt(D_HEAD)
        scores = jnp.einsum('bhqd,bhkd->bhqk', q, k) * scale
        mask = (adj == 0)[None, None, :, :]
        scores = jnp.where(mask, -jnp.inf, scores)
        attn = jax.nn.softmax(scores, axis=-1)
        out = jnp.einsum('bhqk,bhkd->bhqd', attn, v)
        out = out.transpose(0, 2, 1, 3).reshape(b, n, D_MODEL)
        return out @ Wo.T + bo
    x = _layernorm(x + _L0_gnn_ref(x, adj, L0_gnn_W_heads, L0_gnn_a_heads, L0_gnn_W_out, L0_gnn_a_out, L0_gnn_w1, L0_gnn_b1, L0_gnn_w2, L0_gnn_b2, L0_gnn_ln_gamma, L0_gnn_ln_beta), axis=-1)
    x = _layernorm(x + _L1_gnn_ref(x, adj, L1_gnn_Wq, L1_gnn_bq, L1_gnn_Wk, L1_gnn_bk, L1_gnn_Wv, L1_gnn_bv, L1_gnn_Wo, L1_gnn_bo), axis=-1)
    return x

_drawn_inputs = setup_inputs


def setup_inputs(seed=0):
    import zlib

    import numpy as np

    out = dict(_drawn_inputs(seed))
    spreads = {'L0_gnn_b1': (0.0, 0.1),
     'L0_gnn_b2': (0.0, 0.1),
     'L0_gnn_ln_gamma': (1.0, 0.2),
     'L0_gnn_ln_beta': (0.0, 0.1)}
    factors = {'L1_gnn_Wq': 3.324,
     'L1_gnn_bq': 8.0,
     'L1_gnn_Wk': 3.349,
     'L1_gnn_bk': 8.0,
     'L1_gnn_bv': 2.907}
    for name, (base, spread) in spreads.items():
        noise = np.random.default_rng([zlib.crc32(name.encode()), seed]).standard_normal(out[name].shape)
        drawn = base * np.exp(spread * noise) if base else spread * noise
        out[name] = jnp.asarray(drawn.astype(out[name].dtype))
    for name, factor in factors.items():
        out[name] = (out[name] * factor).astype(out[name].dtype)
    return out
```

```python
import concourse.bass as bass
from concourse import mybir
from contextlib import ExitStack


def gat_then_attention_kernel(nc: bass.Bass, x_t, x, adj, w_heads, a_heads, w_out, a_out, w1, b1_cols, w2, b2,
                              ln_gamma, ln_beta, wq_t, bq_cols, wk_t, bk_cols, wv_t, bv, wo_t, bo, identity, out):
    fp32 = mybir.dt.float32
    fp32r = mybir.dt.float32r
    bf16 = mybir.dt.bfloat16
    i32 = mybir.dt.int32
    ALU = mybir.AluOpType
    ACT = mybir.ActivationFunctionType
    AX = mybir.AxisListType

    N = 128
    F = x.shape[2]
    KT = F // 128
    PAIRS = x.shape[0] // 2
    GH = w_heads.shape[0]
    HF = GH * F
    HT = HF // 128
    AH = 8
    D = F // AH
    SCALE = float(D) ** -0.5
    LEAKY = 0.01
    EPS = 1e-5
    MASKED = -1e30
    NF = 2 * GH
    WC = NF + HF
    CH = 3
    CW = WC // CH
    assert CW * CH == WC and CW <= 512
    F2 = F + 2

    ctx = ExitStack()
    with ctx:
        def sb(name, shape, dt=fp32):
            return ctx.enter_context(nc.sbuf_tensor(name, shape, dt))

        def ps(name, shape):
            return ctx.enter_context(nc.psum_tensor(name, shape, fp32))

        def sem(name):
            return ctx.enter_context(nc.semaphore(name))

        ident = sb("ident", [128, 128])
        ident_bf = sb("ident_bf", [128, 128], bf16)
        adj_i = sb("adj_i", [128, N], i32)
        adj_f = sb("adj_f", [128, N])
        gat_mask = sb("gat_mask", [128, N], bf16)
        mha_mask = sb("mha_mask", [128, N], bf16)
        row_ok = sb("row_ok", [128, 3])
        ao_rows = sb("ao_rows", [128, 2 * F])
        small_names = ("w1", "w2", "wq", "wk", "wv", "wo")
        w_hi, w_lo = sb("w_hi", [128, KT, WC], fp32r), sb("w_lo", [128, KT, WC], fp32r)
        wout_hi, wout_lo = sb("wout_hi", [128, HT, F2], fp32r), sb("wout_lo", [128, HT, F2], fp32r)
        small = {k: (sb(k + "_hi", [128, KT, F], fp32r), sb(k + "_lo", [128, KT, F], fp32r)) for k in small_names}
        b1c, bqc, bkc = sb("b1c", [128, KT]), sb("bqc", [128, KT]), sb("bkc", [128, KT])
        b2r, gamr, betr, bvr, bor = (sb(n, [128, F]) for n in ("b2r", "gamr", "betr", "bvr", "bor"))
        neg_half = sb("neg_half", [128, 2])

        xt = sb("xt", [128, KT, 2, N])
        xt_hi, xt_lo = sb("xt_hi", [128, KT, 2, N], fp32r), sb("xt_lo", [128, KT, 2, N], fp32r)
        wh = [sb(f"wh{g}", [128, WC]) for g in range(2)]
        gat_probs = sb("gat_probs", [128, 3 * 2 * GH * N])
        t1, e1, p1 = ([gat_probs[:, (2 * i + g) * GH * N:(2 * i + g + 1) * GH * N].rearrange("p (h m) -> p h m", m=N)
                       for g in range(2)] for i in range(3))
        pt1 = [sb(f"pt1_{g}", [128, GH, N]) for g in range(2)]
        mx1 = [sb(f"mx1_{g}", [128, GH]) for g in range(2)]
        m1 = [sb(f"m1_{g}", [128, GH]) for g in range(2)]
        sum1 = [sb(f"sum1_{g}", [128, GH]) for g in range(2)]
        r1 = [sb(f"r1_{g}", [128, GH]) for g in range(2)]
        elu_in = sb("elu_in", [128, max(2 * HT * N, KT * WC)])
        em = [elu_in[:, g * HT * N:(g + 1) * HT * N].rearrange("p (t n) -> p t n", n=N) for g in range(2)]
        ht_hi = [sb(f"ht_hi{g}", [128, HT, N], fp32r) for g in range(2)]
        ht_lo = [sb(f"ht_lo{g}", [128, HT, N], fp32r) for g in range(2)]
        wh2 = sb("wh2", [128, 2, F2])

        xn = sb("xn", [128, 2, F])
        xb = sb("xb", [128, 2, F])
        t2, e2, p2, pt2 = (sb(n, [128, 2, N]) for n in ("t2", "e2", "p2", "pt2"))
        mx2, m2, sum2, r2 = (sb(n, [128, 2]) for n in ("mx2", "m2", "sum2", "r2"))
        em2, gat, gat_b2 = (sb(n, [128, 2, F]) for n in ("em2", "gat", "gat_b2"))
        gt_hi, gt_lo = sb("gt_hi", [128, KT, 2, N], fp32r), sb("gt_lo", [128, KT, 2, N], fp32r)
        hid = sb("hid", [128, KT, 2, N])
        hid_hi, hid_lo = sb("hid_hi", [128, KT, 2, N], fp32r), sb("hid_lo", [128, KT, 2, N], fp32r)
        y1, z1, x1, x1b = (sb(n, [128, 2, F]) for n in ("y1", "z1", "x1", "x1b"))
        stats = [sb(f"stats{i}", [128, 2, 6]) for i in range(3)]
        mv = [sb(f"mv{i}", [128, 2, 2]) for i in range(3)]
        ve = [sb(f"ve{i}", [128, 2]) for i in range(3)]
        rstd = [sb(f"rstd{i}", [128, 2]) for i in range(3)]
        x1t_hi, x1t_lo = sb("x1t_hi", [128, KT, 2, N], fp32r), sb("x1t_lo", [128, KT, 2, N], fp32r)
        qt, kt = sb("qt", [128, KT, 2, N]), sb("kt", [128, KT, 2, N])
        v = sb("v", [128, 2, F])
        mx3 = [sb(f"mx3_{g}", [128, AH]) for g in range(2)]
        nb3 = [sb(f"nb3_{g}", [128, AH]) for g in range(2)]
        sum3 = [sb(f"sum3_{g}", [128, AH]) for g in range(2)]
        r3 = [sb(f"r3_{g}", [128, AH]) for g in range(2)]
        mha_probs = sb("mha_probs", [128, max(6 * AH * N, 4 * AH * N + HT * F2)])
        e3, p3, pt3 = ([mha_probs[:, (2 * i + g) * AH * N:(2 * i + g + 1) * AH * N].rearrange("p (h m) -> p h m", m=N)
                        for g in range(2)] for i in range(3))
        at_hi, at_lo = sb("at_hi", [128, KT, 2, N], fp32r), sb("at_lo", [128, KT, 2, N], fp32r)
        y3, fin = sb("y3", [128, 2, F]), sb("fin", [128, 2, F])

        small_in = {k: gat_probs[:, i * KT * F:(i + 1) * KT * F].rearrange("p (t o) -> p t o", t=KT)
                    for i, k in enumerate(small_names)}
        w_in = elu_in[:, 0:KT * WC].rearrange("p (t c) -> p t c", t=KT)
        a_rows = mha_probs[:, 0:2 * GH * F].rearrange("p (h j) -> p h j", h=GH)
        prod = mha_probs[:, 2 * GH * F:2 * GH * F + HT * F].rearrange("p (t o) -> p t o", t=HT)
        wout_in = mha_probs[:, 4 * GH * F:4 * GH * F + HT * F2].rearrange("p (t c) -> p t c", t=HT)

        tri = ps("tri", [128, 3, 512])
        mid = ps("mid", [128, 512])
        wide_b = ps("wide_b", [128, 2, 512])
        wide_a = ps("wide_a", [128, 2, 512])
        wide = [wide_a, wide_b]

        def heads(bank):
            return bank.rearrange("p (h m) -> p h m", m=N)

        s1_ps = pt1_ps = heads(mid[:, :])
        wh2_ps = mid[:, 0:F2]
        s2_ps, pt2_ps = heads(wide_b[:, 0, 0:2 * N]), heads(wide_b[:, 1, 0:2 * N])
        gat_ps = wide_a[:, 0, :].rearrange("p (g f) -> p g f", g=2)
        gt_ps = wide_a[:, 1, :].rearrange("p (t g n) -> p t g n", t=KT, g=2)
        hid_ps = wide_b[:, 0, :].rearrange("p (t g n) -> p t g n", t=KT, g=2)
        y1_ps = wide_b[:, 1, :].rearrange("p (g f) -> p g f", g=2)
        x1t_ps = tri[:, 0, :].rearrange("p (t g n) -> p t g n", t=KT, g=2)
        v_ps = tri[:, 0, :].rearrange("p (g f) -> p g f", g=2)
        q_ps = at_ps = tri[:, 1, :].rearrange("p (t g n) -> p t g n", t=KT, g=2)
        k_ps = tri[:, 2, :].rearrange("p (t g n) -> p t g n", t=KT, g=2)
        y3_ps = tri[:, 2, :].rearrange("p (g f) -> p g f", g=2)

        s_adj, s_big, s_small, s_rows, s_cols = (sem("load_" + n) for n in ("adj", "big", "small", "rows", "cols"))
        s_idn, s_const, s_masks, s_dsc, s_wready, s_smallw = (
            sem(n) for n in ("ident_loaded", "constants_ready", "masks_ready", "setup_chain", "weights_ready",
                             "small_weights_ready"))
        s_group = sem("score_row_group_done")
        s_passed = sem("waits_passed")
        s_xt, s_xn, s_store = sem("xt_loaded"), sem("xn_loaded"), sem("out_stored")
        s_xhi, s_xsplit = sem("xt_hi_ready"), sem("xt_split")
        s_whmm, s_wh = sem("wh_mm"), sem("wh_ready")
        s_s1, s_t1, s_mx1, s_lk1, s_m1, s_d1, s_e1 = (
            sem(n) for n in ("s1_mm", "t1_ready", "mx1_ready", "leaky1", "m1_ready", "d1_ready", "e1_ready"))
        s_sum1, s_r1, s_p1, s_pt1mm, s_pt1 = (sem(n) for n in ("sum1", "r1_ready", "p1_ready", "pt1_mm", "pt1_ready"))
        s_htmm, s_eh, s_em, s_h, s_hhi, s_hlo = (
            sem(n) for n in ("ht_mm", "eh_ready", "em_ready", "h_ready", "ht_hi_ready", "ht_lo_ready"))
        s_wh2mm, s_wh2 = sem("wh2_mm"), sem("wh2_ready")
        s_xb = sem("xb_ready")
        s_s2, s_t2, s_mx2, s_lk2, s_m2, s_d2, s_e2, s_sum2, s_r2, s_p2, s_pt2mm, s_pt2 = (
            sem(n) for n in ("s2_mm", "t2_ready", "mx2_ready", "leaky2", "m2_ready", "d2_ready", "e2_ready", "sum2",
                             "r2_ready", "p2_ready", "pt2_mm", "pt2_ready"))
        s_gatmm, s_eo, s_em2, s_gat, s_gatb2, s_gtmm, s_gthi, s_gtlo = (
            sem(n) for n in ("gat_mm", "eo_ready", "em2_ready", "gat_ready", "gat_b2_ready", "gt_mm", "gt_hi_ready",
                             "gt_lo_ready"))
        s_hidmm, s_hid, s_hidhi, s_hidlo, s_y1mm, s_y1 = (
            sem(n) for n in ("hid_mm", "hid_ready", "hid_hi_ready", "hid_lo_ready", "y1_mm", "y1_ready"))
        s_st = [sem(f"stats{i}_ready") for i in range(3)]
        s_mv = [sem(f"mv{i}_ready") for i in range(3)]
        s_ve = [sem(f"var_eps{i}_ready") for i in range(3)]
        s_rstd = [sem(f"rstd{i}_ready") for i in range(3)]
        s_g1, s_z1, s_x1, s_x1b = (sem(n) for n in ("y1_gamma", "z1_ready", "x1_ready", "x1b_ready"))
        s_x1tmm, s_x1thi, s_x1tlo = sem("x1t_mm"), sem("x1t_hi_ready"), sem("x1t_lo_ready")
        s_qmm, s_kmm, s_vmm, s_qt, s_kt, s_v = (
            sem(n) for n in ("q_mm", "k_mm", "v_mm", "q_ready", "k_ready", "v_ready"))
        s_mx3, s_nb3, s_e3, s_ri3, s_r3, s_p3, s_pt3mm, s_pt3 = (
            sem(n) for n in ("mx3_ready", "nb3_ready", "e3_ready", "recip3", "r3_ready", "p3_ready",
                             "pt3_mm", "pt3_ready"))
        s_atmm, s_athi, s_atlo, s_y3mm, s_y3, s_fin = (
            sem(n) for n in ("at_mm", "at_hi_ready", "at_lo_ready", "y3_mm", "y3_ready", "fin_ready"))

        def wait(eng, semaphore, value):
            if not isinstance(value, int) or value > 0:
                eng.wait_ge(semaphore, value)

        def wait_apart(eng, semaphore, value):
            wait(eng, semaphore, value)
            eng.sem_inc(s_passed, 1)

        def per_head(column, n=N):
            return column.unsqueeze(2).to_broadcast([128, column.shape[1], n])

        def run_steps(eng, step):
            step(0, True, False)
            step(1, True, True)
            with eng.Fori(2, PAIRS - 2) as s:
                step(s, True, True)
            step(PAIRS - 2, True, True)
            step(PAIRS - 1, True, True)
            step(PAIRS, False, True)

        block = ctx.enter_context(nc.Block())

        @block.sync
        def _(sp):
            def load_xt(p):
                wait(sp, s_xsplit, p)
                sp.dma_start(xt[:, :, :, :], x_t[p]).then_inc(s_xt, 16)

            sp.dma_start(adj_i[:, :], adj).then_inc(s_adj, 16)
            sp.dma_start(ident[:, :], identity).then_inc(s_idn, 16)
            load_xt(0)
            sp.dma_start(a_rows[:, :, :], a_heads.unsqueeze(0).to_broadcast([128, GH, 2 * F])).then_inc(s_big, 16)
            for k in range(KT):
                sp.dma_start(w_in[:, k, NF:].rearrange("p (h o) -> p h o", h=GH),
                             w_heads[:, k * 128:(k + 1) * 128, :].rearrange("h p o -> p h o")).then_inc(s_big, 16)
            sp.dma_start(ao_rows[:, :], a_out.unsqueeze(0).to_broadcast([128, 2 * F])).then_inc(s_big, 16)
            sp.dma_start(wout_in[:, :, 0:F], w_out.rearrange("(t p) o -> p t o", p=128)).then_inc(s_big, 16)
            for name, w in (("w1", w1), ("w2", w2), ("wq", wq_t), ("wk", wk_t), ("wv", wv_t), ("wo", wo_t)):
                sp.dma_start(small_in[name][:, :, :], w.rearrange("(t p) o -> p t o", p=128)).then_inc(s_small, 16)
            for dst, src in ((b1c, b1_cols), (bqc, bq_cols), (bkc, bk_cols)):
                sp.dma_start(dst[:, :], src).then_inc(s_cols, 16)
            for dst, src in ((b2r, b2), (gamr, ln_gamma), (betr, ln_beta), (bvr, bv), (bor, bo)):
                sp.dma_start(dst[:, :], src.unsqueeze(0).to_broadcast([128, F])).then_inc(s_rows, 16)

            def step(s, front, back):
                if front:
                    if not isinstance(s, int) or s + 1 < PAIRS:
                        load_xt(s + 1)
                    wait(sp, s_xb, s)
                    sp.dma_start(xn[:, :, :], x[bass.ds(2 * s, 2)].rearrange("g n f -> n g f")).then_inc(s_xn, 16)
                if back:
                    sp.wait_ge(s_fin, 2 * s)
                    sp.dma_start(out[bass.ds(2 * s - 2, 2)].rearrange("g n f -> n g f"), fin[:, :, :]).then_inc(s_store, 16)

            run_steps(sp, step)
            sp.wait_ge(s_store, 16 * PAIRS)

        @block.tensor
        def _(pe):
            def split_mm(dst, hi_l, lo_l, hi_r, lo_r, first, last):
                nc.tensor.matmul(dst, lo_l, hi_r, start=first, stop=False)
                nc.tensor.matmul(dst, hi_l, lo_r, start=False, stop=False)
                return nc.tensor.matmul(dst, hi_l, hi_r, start=False, stop=last)

            def first_features(p, g, c):
                if g == 0 and c == 0:
                    pe.wait_ge(s_xsplit, p + 1)
                    wait(pe, s_v, p - 1)
                if g == 0 and c == 1:
                    wait(pe, s_atlo, p - 1)
                if g == 0 and c == 2:
                    wait(pe, s_y3, p - 1)
                if g == 1:
                    pe.wait_ge(s_wh, 6 * p + c + 1)
                for k in range(KT):
                    cols = slice(c * CW, (c + 1) * CW)
                    last = split_mm(tri[:, c, 0:CW], xt_hi[:, k, g, :], xt_lo[:, k, g, :], w_hi[:, k, cols],
                                    w_lo[:, k, cols], k == 0, k == KT - 1)
                last.then_inc(s_whmm, 1)

            def gat_scores1(p, g):
                pe.wait_ge(s_wh, 6 * p + 3 * g + 1)
                if g == 0:
                    wait(pe, s_wh2, 2 * p)
                else:
                    pe.wait_ge(s_t1, 2 * p + 1)
                nc.tensor.matmul(s1_ps, ident_bf[:, :], gat_mask[:, :].unsqueeze(1).to_broadcast([128, GH, N]),
                                 start=True, stop=False)
                for h in range(GH):
                    last = nc.tensor.matmul(s1_ps[:, h, :], wh[g][:, GH + h:GH + h + 1].to_broadcast([128, 128]),
                                            ident[:, :], is_transpose=True, start=False, stop=(h == GH - 1))
                last.then_inc(s_s1, 1)

            def transpose_p1(p, g):
                pe.wait_ge(s_p1, 2 * p + g + 1)
                if g == 0:
                    pe.wait_ge(s_t1, 2 * p + 2)
                else:
                    pe.wait_ge(s_pt1, 2 * p + 1)
                for h in range(GH):
                    last = nc.tensor.transpose(pt1_ps[:, h, :], p1[g][:, h, :], ident[:, :])
                last.then_inc(s_pt1mm, 1)

            def gat_values1(p, g):
                pe.wait_ge(s_pt1, 2 * p + g + 1)
                pe.wait_ge(s_wh, 6 * p + 3 * g + 3)
                if g == 0:
                    wait(pe, s_gtlo, p)
                else:
                    wait(pe, s_y1, p)
                for t in range(HT):
                    dst = wide[g][:, t // 4, (t % 4) * N:(t % 4 + 1) * N]
                    last = nc.tensor.matmul(dst, wh[g][:, NF + t * 128:NF + (t + 1) * 128], pt1[g][:, t // KT, :],
                                            start=True, stop=True)
                    if t % 4 == 3:
                        last.then_inc(s_htmm, 1)

            def second_features(p, g):
                pe.wait_ge(s_hhi, 2 * p + g + 1)
                pe.wait_ge(s_hlo, 2 * p + g + 1)
                if g == 0:
                    pe.wait_ge(s_pt1, 2 * p + 2)
                else:
                    pe.wait_ge(s_wh2, 2 * p + 1)
                for t in range(HT):
                    last = split_mm(wh2_ps, ht_hi[g][:, t, :], ht_lo[g][:, t, :], wout_hi[:, t, :], wout_lo[:, t, :],
                                    t == 0, t == HT - 1)
                last.then_inc(s_wh2mm, 1)

            def gat_scores2(q):
                pe.wait_ge(s_wh2, 2 * q + 2)
                wait(pe, s_pt3, 4 * q)
                nc.tensor.matmul(s2_ps, ident_bf[:, :], gat_mask[:, :].unsqueeze(1).to_broadcast([128, 2, N]),
                                 start=True, stop=False)
                for g in range(2):
                    last = nc.tensor.matmul(s2_ps[:, g, :], wh2[:, g, F + 1:F + 2].to_broadcast([128, 128]),
                                            ident[:, :], is_transpose=True, start=False, stop=(g == 1))
                last.then_inc(s_s2, 1)

            def transpose_p2(q):
                pe.wait_ge(s_p2, q + 1)
                for g in range(2):
                    last = nc.tensor.transpose(pt2_ps[:, g, :], p2[:, g, :], ident[:, :])
                last.then_inc(s_pt2mm, 1)

            def gat_values2(q):
                pe.wait_ge(s_pt2, q + 1)
                for g in range(2):
                    last = nc.tensor.matmul(gat_ps[:, g, :], pt2[:, g, :], wh2[:, g, 0:F], start=True, stop=True)
                last.then_inc(s_gatmm, 1)

            def transpose_gat(q):
                pe.wait_ge(s_gat, q + 1)
                for t in range(KT):
                    for g in range(2):
                        last = nc.tensor.transpose(gt_ps[:, t, g, :], gat[:, g, t * 128:(t + 1) * 128], ident[:, :])
                last.then_inc(s_gtmm, 1)

            def transposed_product(dst, weight, hi, lo):
                w_h, w_l = small[weight]
                for m in range(KT):
                    for k in range(KT):
                        last = split_mm(dst[:, m, :, :], w_h[:, k, m * 128:(m + 1) * 128],
                                        w_l[:, k, m * 128:(m + 1) * 128], hi[:, k, :, :], lo[:, k, :, :],
                                        k == 0, k == KT - 1)
                return last

            def natural_product(dst, weight, hi, lo):
                w_h, w_l = small[weight]
                for g in range(2):
                    for k in range(KT):
                        last = split_mm(dst[:, g, :], hi[:, k, g, :], lo[:, k, g, :], w_h[:, k, :], w_l[:, k, :],
                                        k == 0, k == KT - 1)
                return last

            def ffn_up(q):
                pe.wait_ge(s_gthi, q + 1)
                pe.wait_ge(s_gtlo, q + 1)
                transposed_product(hid_ps, "w1", gt_hi, gt_lo).then_inc(s_hidmm, 1)

            def ffn_down(q):
                pe.wait_ge(s_hidhi, q + 1)
                pe.wait_ge(s_hidlo, q + 1)
                natural_product(y1_ps, "w2", hid_hi, hid_lo).then_inc(s_y1mm, 1)

            def transpose_x1(q):
                pe.wait_ge(s_x1, 2 * q + 2)
                for t in range(KT):
                    for g in range(2):
                        last = nc.tensor.transpose(x1t_ps[:, t, g, :], x1[:, g, t * 128:(t + 1) * 128], ident[:, :])
                last.then_inc(s_x1tmm, 1)

            def qkv(q):
                pe.wait_ge(s_x1thi, q + 1)
                pe.wait_ge(s_x1tlo, q + 1)
                transposed_product(q_ps, "wq", x1t_hi, x1t_lo).then_inc(s_qmm, 1)
                transposed_product(k_ps, "wk", x1t_hi, x1t_lo).then_inc(s_kmm, 1)
                natural_product(v_ps, "wv", x1t_hi, x1t_lo).then_inc(s_vmm, 1)

            def mha_scores(q, g, p_done):
                pe.wait_ge(s_qt, 2 * q + 2)
                pe.wait_ge(s_kt, 2 * q + 2)
                if p_done is not None:
                    pe.wait_ge(s_h, 4 * p_done + 2 * g + 2)
                for b in range(2):
                    nc.tensor.matmul(heads(wide[g][:, b, :]), ident_bf[:, :],
                                     mha_mask[:, :].unsqueeze(1).to_broadcast([128, 4, N]), start=True, stop=False,
                                     skip_group_check=True)
                for r in range(4):
                    rows = slice(32 * r, 32 * r + 32)
                    if r >= 2:
                        pe.wait_ge(s_group, 8 * q + 4 * g + r - 1)
                    for t in range(KT):
                        b, c = head_place(r, t)
                        last = nc.tensor.matmul(wide[g][:, b, c * N:(c + 1) * N], qt[rows, t, g, :], kt[rows, t, g, :],
                                                start=False, stop=(r >= 2 and t == KT - 1), skip_group_check=True)
                    last.then_inc(s_group, 1)

            def transpose_p3(q, g):
                for b in range(2):
                    pe.wait_ge(s_p3, 4 * q + 2 * g + b + 1)
                    for c in range(4):
                        last = nc.tensor.transpose(wide[g][:, b, c * N:(c + 1) * N], p3[g][:, 4 * b + c, :], ident[:, :])
                    last.then_inc(s_pt3mm, 1)

            def mha_values(q):
                pe.wait_ge(s_v, q + 1)
                for g in range(2):
                    pe.wait_ge(s_pt3, 4 * q + 2 * g + 2)
                    for t in range(KT):
                        for r in range(4):
                            b, c = head_place(r, t)
                            head = 4 * t + r
                            last = nc.tensor.matmul(at_ps[32 * r:32 * r + 32, t, g, :], v[:, g, head * D:(head + 1) * D],
                                                    pt3[g][:, 4 * b + c, :], start=True, stop=True)
                last.then_inc(s_atmm, 1)

            def out_projection(q):
                pe.wait_ge(s_athi, q + 1)
                pe.wait_ge(s_atlo, q + 1)
                natural_product(y3_ps, "wo", at_hi, at_lo).then_inc(s_y3mm, 1)

            def head_place(r, t):
                return r % 2, 2 * (r // 2) + t

            pe.wait_ge(s_idn, 16)
            pe.wait_ge(s_masks, 3)
            pe.wait_ge(s_wready, 2)
            pe.wait_ge(s_smallw, len(small))

            def step(s, front, back):
                q = s - 1
                if back:
                    gat_scores2(q)
                if front:
                    for c in range(CH):
                        first_features(s, 0, c)
                    gat_scores1(s, 0)
                if back:
                    transpose_p2(q)
                if front:
                    first_features(s, 1, 0)
                if back:
                    gat_values2(q)
                if front:
                    first_features(s, 1, 1)
                if back:
                    transpose_gat(q)
                if front:
                    first_features(s, 1, 2)
                    gat_scores1(s, 1)
                if back:
                    ffn_up(q)
                if front:
                    transpose_p1(s, 0)
                if back:
                    ffn_down(q)
                if front:
                    gat_values1(s, 0)
                    transpose_p1(s, 1)
                    gat_values1(s, 1)
                if back:
                    transpose_x1(q)
                    qkv(q)
                    mha_scores(q, 0, s if front else None)
                if front:
                    second_features(s, 0)
                if back:
                    mha_scores(q, 1, s if front else None)
                if front:
                    second_features(s, 1)
                if back:
                    transpose_p3(q, 0)
                    transpose_p3(q, 1)
                    mha_values(q)
                    out_projection(q)

            run_steps(pe, step)

        @block.scalar
        def _(act):
            def wh_out(p, g, c):
                act.wait_ge(s_whmm, 6 * p + 3 * g + c + 1)
                wait(act, s_htmm, 4 * (p - 1) + 2 * g + 2)
                nc.scalar.activation(wh[g][:, c * CW:(c + 1) * CW], tri[:, c, 0:CW], ACT.Copy).then_inc(s_wh, 1)

            def exp1(p, g):
                act.wait_ge(s_d1, 2 * p + g + 1)
                nc.scalar.activation(e1[g][:, :, :], e1[g][:, :, :], ACT.Exp).then_inc(s_e1, 1)

            def pt1_out(p, g):
                act.wait_ge(s_pt1mm, 2 * p + g + 1)
                nc.scalar.activation(pt1[g][:, :, :], pt1_ps, ACT.Copy).then_inc(s_pt1, 1)

            def exp_values1(p, g):
                wait(act, s_hlo, 2 * (p - 1) + g + 1)
                for b in range(2):
                    act.wait_ge(s_htmm, 4 * p + 2 * g + b + 1)
                    nc.scalar.activation(em[g][:, 4 * b:4 * b + 4, :], heads(wide[g][:, b, :]), ACT.Exp).then_inc(s_eh, 1)

            def wh2_out(p, g):
                act.wait_ge(s_wh2mm, 2 * p + g + 1)
                nc.scalar.activation(wh2[:, g, :], wh2_ps, ACT.Copy).then_inc(s_wh2, 1)

            def exp2(q):
                act.wait_ge(s_d2, q + 1)
                nc.scalar.activation(e2[:, :, :], e2[:, :, :], ACT.Exp).then_inc(s_e2, 1)

            def pt2_out(q):
                act.wait_ge(s_pt2mm, q + 1)
                nc.scalar.activation(pt2[:, :, :], pt2_ps, ACT.Copy).then_inc(s_pt2, 1)

            def exp_gat(q):
                act.wait_ge(s_gatmm, q + 1)
                nc.scalar.activation(em2[:, :, :], gat_ps, ACT.Exp).then_inc(s_eo, 1)

            def gt_hi_out(q):
                act.wait_ge(s_gtmm, q + 1)
                nc.scalar.activation(gt_hi[:, :, :, :], gt_ps, ACT.Copy).then_inc(s_gthi, 1)

            def hidden_out(q):
                act.wait_ge(s_hidmm, q + 1)
                for t in range(KT):
                    nc.scalar.activation(hid[:, t, :, :], hid_ps[:, t, :, :], ACT.Relu, bias=b1c[:, t:t + 1]).then_inc(s_hid, 1)

            def x1t_hi_out(q):
                act.wait_ge(s_x1tmm, q + 1)
                nc.scalar.activation(x1t_hi[:, :, :, :], x1t_ps, ACT.Copy).then_inc(s_x1thi, 1)

            def qk_out(q):
                for mm, src, bias, dst, done in ((s_qmm, q_ps, bqc, qt, s_qt), (s_kmm, k_ps, bkc, kt, s_kt)):
                    act.wait_ge(mm, q + 1)
                    for t in range(KT):
                        nc.scalar.activation(dst[:, t, :, :], src[:, t, :, :], ACT.Identity,
                                             bias=bias[:, t:t + 1]).then_inc(done, 1)

            def exp3(q, g):
                act.wait_ge(s_nb3, 2 * q + g + 1)
                for i in range(AH):
                    nc.scalar.activation(e3[g][:, i, :], wide[g][:, i // 4, (i % 4) * N:(i % 4 + 1) * N], ACT.Exp,
                                         scale=SCALE, bias=nb3[g][:, i:i + 1],
                                         accum_out=sum3[g][:, i:i + 1]).then_inc(s_e3, 1)

            def pt3_out(q, g):
                for b in range(2):
                    act.wait_ge(s_pt3mm, 4 * q + 2 * g + b + 1)
                    nc.scalar.activation(pt3[g][:, 4 * b:4 * b + 4, :], heads(wide[g][:, b, :]), ACT.Copy).then_inc(s_pt3, 1)

            def at_hi_out(q):
                act.wait_ge(s_atmm, q + 1)
                nc.scalar.activation(at_hi[:, :, :, :], at_ps, ACT.Copy).then_inc(s_athi, 1)

            act.wait_ge(s_cols, 48)

            def step(s, front, back):
                q = s - 1
                if front:
                    wh_out(s, 0, 0)
                if front:
                    wh_out(s, 0, 1)
                if back:
                    exp2(q)
                if front:
                    wh_out(s, 0, 2)
                if back:
                    pt2_out(q)
                if front:
                    wh_out(s, 1, 0)
                if back:
                    exp_gat(q)
                if front:
                    exp1(s, 0)
                    wh_out(s, 1, 1)
                if back:
                    gt_hi_out(q)
                if front:
                    wh_out(s, 1, 2)
                if back:
                    hidden_out(q)
                if front:
                    exp1(s, 1)
                    pt1_out(s, 0)
                    exp_values1(s, 0)
                    pt1_out(s, 1)
                    exp_values1(s, 1)
                if back:
                    x1t_hi_out(q)
                    qk_out(q)
                    exp3(q, 0)
                if front:
                    wh2_out(s, 0)
                if back:
                    exp3(q, 1)
                if front:
                    wh2_out(s, 1)
                if back:
                    pt3_out(q, 0)
                    pt3_out(q, 1)
                    at_hi_out(q)

            run_steps(act, step)

        @block.vector
        def _(dve):
            V = nc.vector
            chain = [0]

            def link(ins):
                chain[0] += 1
                ins.then_inc(s_dsc, 1)
                dve.wait_ge(s_dsc, chain[0])

            def split(src, hi, lo, done):
                link(V.tensor_copy(hi, src))
                V.tensor_tensor(lo, src, hi.bitcast(fp32), ALU.subtract).then_inc(done, 1)

            def split_xt(p):
                dve.wait_ge(s_xt, 16 * (p + 1))
                wait(dve, s_whmm, 6 * p)
                V.tensor_copy(xt_hi[:, :, :, :], xt[:, :, :, :]).then_inc(s_xhi, 1)
                dve.wait_ge(s_xhi, p + 1)
                V.tensor_tensor(xt_lo[:, :, :, :], xt[:, :, :, :], xt_hi[:, :, :, :].bitcast(fp32),
                                ALU.subtract).then_inc(s_xsplit, 1)

            def leaky(dst, src, done):
                V.scalar_tensor_tensor(out=dst, in0=src, scalar=LEAKY, in1=src, op0=ALU.mult,
                                       op1=ALU.max).then_inc(done, 1)

            def scores1(p, g):
                dve.wait_ge(s_s1, 2 * p + g + 1)
                V.tensor_tensor(t1[g][:, :, :], s1_ps, per_head(wh[g][:, 0:GH]), ALU.add).then_inc(s_t1, 1)
                dve.wait_ge(s_t1, 2 * p + g + 1)
                V.reduce_max(mx1[g][:, :], t1[g][:, :, :], AX.X).then_inc(s_mx1, 1)
                wait(dve, s_p1, 2 * (p - 1) + g + 1)
                leaky(e1[g][:, :, :], t1[g][:, :, :], s_lk1)
                dve.wait_ge(s_mx1, 2 * p + g + 1)
                leaky(m1[g][:, :], mx1[g][:, :], s_m1)

            def sums1(p, g):
                dve.wait_ge(s_e1, 2 * p + g + 1)
                V.reduce_sum(sum1[g][:, :], e1[g][:, :, :], AX.X).then_inc(s_sum1, 1)
                dve.wait_ge(s_sum1, 2 * p + g + 1)
                wait(dve, s_p1, 2 * (p - 1) + g + 1)
                V.reciprocal(r1[g][:, :], sum1[g][:, :]).then_inc(s_r1, 1)

            def elu1(p, g):
                for b in range(2):
                    part = em[g][:, 4 * b:4 * b + 4, :]
                    dve.wait_ge(s_eh, 4 * p + 2 * g + b + 1)
                    V.tensor_scalar(part, part, 1.0, -1.0, ALU.min, ALU.add).then_inc(s_em, 1)
                for b in range(2):
                    part = em[g][:, 4 * b:4 * b + 4, :]
                    dve.wait_ge(s_em, 4 * p + 2 * g + b + 1)
                    V.tensor_tensor(part, heads(wide[g][:, b, :]), part, ALU.max).then_inc(s_h, 1)

            def elu1_tail(p, g):
                dve.wait_ge(s_hhi, 2 * p + g + 1)
                V.tensor_tensor(ht_lo[g][:, :, :], em[g][:, :, :], ht_hi[g][:, :, :].bitcast(fp32),
                                ALU.subtract).then_inc(s_hlo, 1)

            def scores2(q):
                dve.wait_ge(s_s2, q + 1)
                V.tensor_tensor(t2[:, :, :], s2_ps, wh2[:, :, F:F + 1].to_broadcast([128, 2, N]), ALU.add).then_inc(s_t2, 1)
                dve.wait_ge(s_t2, q + 1)
                V.reduce_max(mx2[:, :], t2[:, :, :], AX.X).then_inc(s_mx2, 1)
                leaky(e2[:, :, :], t2[:, :, :], s_lk2)
                dve.wait_ge(s_mx2, q + 1)
                leaky(m2[:, :], mx2[:, :], s_m2)

            def less_max2(q):
                dve.wait_ge(s_lk2, q + 1)
                dve.wait_ge(s_m2, q + 1)
                V.tensor_tensor(e2[:, :, :], e2[:, :, :], per_head(m2[:, :]), ALU.subtract).then_inc(s_d2, 1)

            def sums2(q):
                dve.wait_ge(s_e2, q + 1)
                V.reduce_sum(sum2[:, :], e2[:, :, :], AX.X).then_inc(s_sum2, 1)
                dve.wait_ge(s_sum2, q + 1)
                V.reciprocal(r2[:, :], sum2[:, :]).then_inc(s_r2, 1)

            def elu2(q):
                dve.wait_ge(s_eo, q + 1)
                V.tensor_scalar(em2[:, :, :], em2[:, :, :], 1.0, -1.0, ALU.min, ALU.add).then_inc(s_em2, 1)
                dve.wait_ge(s_em2, q + 1)
                V.tensor_tensor(gat[:, :, :], gat_ps, em2[:, :, :], ALU.max).then_inc(s_gat, 1)

            def tail_out(q, head_ready, src, hi, lo, done):
                dve.wait_ge(head_ready, q + 1)
                V.tensor_tensor(lo[:, :, :, :], src, hi[:, :, :, :].bitcast(fp32), ALU.subtract).then_inc(done, 1)

            def hidden_tail(q):
                dve.wait_ge(s_hidhi, q + 1)
                V.tensor_tensor(hid_lo[:, :, :, :], hid[:, :, :, :], hid_hi[:, :, :, :].bitcast(fp32),
                                ALU.subtract).then_inc(s_hidlo, 1)

            def norm_stats(i, q, src, ready, count):
                for g in range(2):
                    dve.wait_ge(ready, count * q + (g + 1 if count == 2 else 1))
                    V.bn_stats(stats[i][:, g, :], src[:, g, :]).then_inc(s_st[i], 1)
                wait_apart(dve, s_st[i], 2 * q + 2)
                for g in range(2):
                    V.bn_aggr(mv[i][:, g, :], stats[i][:, g, :]).then_inc(s_mv[i], 1)
                dve.wait_ge(s_mv[i], 2 * q + 2)
                V.tensor_scalar(ve[i][:, :], mv[i][:, :, 1], EPS, None, ALU.add).then_inc(s_ve[i], 1)

            def gat_norms(q):
                dve.wait_ge(s_y1mm, q + 1)
                dve.wait_ge(s_gatb2, q + 1)
                V.tensor_tensor(y1[:, :, :], y1_ps, gat_b2[:, :, :], ALU.add).then_inc(s_y1, 1)
                norm_stats(0, q, y1, s_y1, 1)
                for g in range(2):
                    V.scalar_tensor_tensor(out=y1[:, g, :], in0=y1[:, g, :], scalar=mv[0][:, g, 0:1], in1=gamr[:, :],
                                           op0=ALU.subtract, op1=ALU.mult).then_inc(s_g1, 1)
                dve.wait_ge(s_rstd[0], q + 1)
                dve.wait_ge(s_xb, q + 1)
                for g in range(2):
                    dve.wait_ge(s_g1, 2 * q + g + 1)
                    V.scalar_tensor_tensor(out=z1[:, g, :], in0=y1[:, g, :], scalar=rstd[0][:, g:g + 1],
                                           in1=xb[:, g, :], op0=ALU.mult, op1=ALU.add).then_inc(s_z1, 1)
                norm_stats(1, q, z1, s_z1, 2)
                dve.wait_ge(s_rstd[1], q + 1)
                for g in range(2):
                    V.tensor_scalar(x1[:, g, :], z1[:, g, :], mv[1][:, g, 0:1], rstd[1][:, g:g + 1], ALU.subtract,
                                    ALU.mult).then_inc(s_x1, 1)

            def v_out(q):
                dve.wait_ge(s_vmm, q + 1)
                V.tensor_tensor(v[:, :, :], v_ps, bvr[:, :].unsqueeze(1).to_broadcast([128, 2, F]),
                                ALU.add).then_inc(s_v, 1)

            def max3(q, g):
                dve.wait_ge(s_group, 8 * q + 4 * g + 4)
                V.reduce_max(mx3[g][:, :], wide[g][:, :, :].rearrange("p b (c m) -> p (b c) m", m=N), AX.X).then_inc(s_mx3, 1)
                dve.wait_ge(s_mx3, 2 * q + g + 1)
                V.tensor_scalar(nb3[g][:, :], mx3[g][:, :], -SCALE, None, ALU.mult).then_inc(s_nb3, 1)

            def recip3(q, g):
                dve.wait_ge(s_e3, AH * (2 * q + g + 1))
                V.reciprocal(r3[g][:, :], sum3[g][:, :]).then_inc(s_ri3, 1)
                dve.wait_ge(s_ri3, 2 * q + g + 1)
                V.tensor_scalar(r3[g][:, :], r3[g][:, :], row_ok[:, 2:3], None, ALU.mult).then_inc(s_r3, 1)

            def final_norm(q):
                dve.wait_ge(s_y3mm, q + 1)
                dve.wait_ge(s_x1b, q + 1)
                V.tensor_tensor(y3[:, :, :], y3_ps, x1b[:, :, :], ALU.add).then_inc(s_y3, 1)
                norm_stats(2, q, y3, s_y3, 1)
                dve.wait_ge(s_rstd[2], q + 1)
                wait(dve, s_store, 16 * q)
                for g in range(2):
                    V.tensor_scalar(fin[:, g, :], y3[:, g, :], mv[2][:, g, 0:1], rstd[2][:, g:g + 1], ALU.subtract,
                                    ALU.mult).then_inc(s_fin, 1)

            V.memset(neg_half[:, :], -0.5).then_inc(s_const, 1)
            dve.wait_ge(s_idn, 16)
            V.tensor_copy(ident_bf[:, :], ident[:, :]).then_inc(s_masks, 1)
            dve.wait_ge(s_adj, 16)
            link(V.tensor_copy(adj_f[:, :], adj_i[:, :]))
            V.tensor_scalar(gat_mask[:, :], adj_f[:, :], 0.0, MASKED, ALU.is_le, ALU.mult).then_inc(s_masks, 1)
            V.tensor_scalar(mha_mask[:, :], adj_f[:, :], 0.0, MASKED, ALU.is_equal, ALU.mult).then_inc(s_masks, 1)
            link(V.tensor_scalar(adj_f[:, :], adj_f[:, :], 0.0, None, ALU.not_equal))
            link(V.reduce_max(row_ok[:, 0:1], adj_f[:, :], AX.X))
            link(V.reciprocal(row_ok[:, 1:2], row_ok[:, 0:1]))
            link(V.tensor_tensor(row_ok[:, 2:3], row_ok[:, 0:1], row_ok[:, 1:2], ALU.mult))
            dve.wait_ge(s_big, 80)
            for k in range(KT):
                for j in range(2):
                    view = prod[:, 0:GH, :]
                    link(V.tensor_tensor(view, w_in[:, k, NF:].rearrange("p (h o) -> p h o", h=GH),
                                         a_rows[:, :, j * F:(j + 1) * F], ALU.mult))
                    link(V.reduce_sum(w_in[:, k, j * GH:(j + 1) * GH], view, AX.X))
            split(w_in[:, :, :], w_hi[:, :, :], w_lo[:, :, :], s_wready)
            split_xt(0)
            for j in range(2):
                link(V.tensor_tensor(prod[:, :, :], wout_in[:, :, 0:F],
                                     ao_rows[:, j * F:(j + 1) * F].unsqueeze(1).to_broadcast([128, HT, F]), ALU.mult))
                link(V.reduce_sum(wout_in[:, :, F + j:F + j + 1], prod[:, :, :], AX.X))
            split(wout_in[:, :, :], wout_hi[:, :, :], wout_lo[:, :, :], s_wready)
            dve.wait_ge(s_small, 16 * len(small))
            for name, (hi, lo) in small.items():
                split(small_in[name][:, :, :], hi[:, :, :], lo[:, :, :], s_smallw)
            dve.wait_ge(s_rows, 80)

            def step(s, front, back):
                q = s - 1
                more = front and (not isinstance(s, int) or s + 1 < PAIRS)
                if back:
                    scores2(q)
                    less_max2(q)
                    sums2(q)
                if front:
                    scores1(s, 0)
                if back:
                    elu2(q)
                if front:
                    sums1(s, 0)
                if back:
                    tail_out(q, s_gthi, gt_ps, gt_hi, gt_lo, s_gtlo)
                if front:
                    scores1(s, 1)
                if back:
                    hidden_tail(q)
                if front:
                    sums1(s, 1)
                if back:
                    gat_norms(q)
                if front:
                    elu1(s, 0)
                    elu1_tail(s, 0)
                if back:
                    tail_out(q, s_x1thi, x1t_ps, x1t_hi, x1t_lo, s_x1tlo)
                if front:
                    elu1(s, 1)
                    elu1_tail(s, 1)
                if back:
                    v_out(q)
                    max3(q, 0)
                if more:
                    split_xt(s + 1)
                if back:
                    max3(q, 1)
                    recip3(q, 0)
                    recip3(q, 1)
                    tail_out(q, s_athi, at_ps, at_hi, at_lo, s_atlo)
                    final_norm(q)

            run_steps(dve, step)

        @block.gpsimd
        def _(pool):
            P = nc.gpsimd

            def x_beta(q):
                pool.wait_ge(s_xn, 16 * (q + 1))
                wait(pool, s_z1, 2 * q)
                P.tensor_tensor(xb[:, :, :], xn[:, :, :], betr[:, :].unsqueeze(1).to_broadcast([128, 2, F]),
                                ALU.add).then_inc(s_xb, 1)

            def less_max1(p, g):
                pool.wait_ge(s_lk1, 2 * p + g + 1)
                pool.wait_ge(s_m1, 2 * p + g + 1)
                P.tensor_tensor(e1[g][:, :, :], e1[g][:, :, :], per_head(m1[g][:, :]), ALU.subtract).then_inc(s_d1, 1)

            def normalise1(p, g):
                pool.wait_ge(s_r1, 2 * p + g + 1)
                wait(pool, s_pt1mm, 2 * (p - 1) + g + 1)
                P.tensor_tensor(p1[g][:, :, :], e1[g][:, :, :], per_head(r1[g][:, :]), ALU.mult).then_inc(s_p1, 1)

            def elu1_head(p, g):
                wait(pool, s_wh2mm, 2 * (p - 1) + g + 1)
                wait_apart(pool, s_h, 4 * p + 2 * g + 2)
                P.tensor_scalar(ht_hi[g][:, :, :], em[g][:, :, :], 1.0, 1.0, ALU.mult, ALU.mult).then_inc(s_hhi, 1)

            def normalise2(q):
                pool.wait_ge(s_r2, q + 1)
                P.tensor_tensor(p2[:, :, :], e2[:, :, :], per_head(r2[:, :]), ALU.mult).then_inc(s_p2, 1)

            def gat_plus_b2(q):
                pool.wait_ge(s_gat, q + 1)
                P.tensor_tensor(gat_b2[:, :, :], gat[:, :, :], b2r[:, :].unsqueeze(1).to_broadcast([128, 2, F]),
                                ALU.add).then_inc(s_gatb2, 1)

            def hidden_head(q):
                wait_apart(pool, s_hid, 2 * q + 2)
                P.tensor_scalar(hid_hi[:, :, :, :], hid[:, :, :, :], 1.0, 1.0, ALU.mult, ALU.mult).then_inc(s_hidhi, 1)

            def inverse_std(i, q):
                pool.wait_ge(s_ve[i], q + 1)
                P.tensor_tensor(rstd[i][:, :], ve[i][:, :], neg_half[:, :], ALU.pow).then_inc(s_rstd[i], 1)

            def x1_plus_bo(q):
                pool.wait_ge(s_x1, 2 * q + 2)
                P.tensor_tensor(x1b[:, :, :], x1[:, :, :], bor[:, :].unsqueeze(1).to_broadcast([128, 2, F]),
                                ALU.add).then_inc(s_x1b, 1)

            def normalise3(q, g):
                pool.wait_ge(s_r3, 2 * q + g + 1)
                for b in range(2):
                    part = slice(4 * b, 4 * b + 4)
                    P.tensor_tensor(p3[g][:, part, :], e3[g][:, part, :], per_head(r3[g][:, part]),
                                    ALU.mult).then_inc(s_p3, 1)

            pool.wait_ge(s_rows, 80)
            pool.wait_ge(s_const, 1)

            def step(s, front, back):
                q = s - 1
                if back:
                    x_beta(q)
                    normalise2(q)
                if front:
                    less_max1(s, 0)
                    normalise1(s, 0)
                if back:
                    gat_plus_b2(q)
                if front:
                    less_max1(s, 1)
                if back:
                    hidden_head(q)
                if front:
                    normalise1(s, 1)
                if back:
                    inverse_std(0, q)
                    inverse_std(1, q)
                    x1_plus_bo(q)
                if front:
                    elu1_head(s, 0)
                    elu1_head(s, 1)
                if back:
                    normalise3(q, 0)
                    normalise3(q, 1)
                    inverse_std(2, q)

            run_steps(pool, step)


def kernel(**inputs):
    import numpy as np
    import concourse.bacc as bacc
    from concourse import mybir as mb
    from concourse.bass_utils import run_bass_kernel_spmd

    a = {k: np.ascontiguousarray(v) for k, v in inputs.items()}
    x = a["x"]
    B, n, f = x.shape

    def columns(v):
        return np.ascontiguousarray(v.reshape(-1, 128).T)

    arrays = {
        "x_t": np.ascontiguousarray(x.reshape(B // 2, 2, n, f // 128, 128).transpose(0, 4, 3, 1, 2)),
        "x": x,
        "adj": a["adj"],
        "w_heads": a["L0_gnn_W_heads"],
        "a_heads": a["L0_gnn_a_heads"],
        "w_out": a["L0_gnn_W_out"],
        "a_out": a["L0_gnn_a_out"],
        "w1": a["L0_gnn_w1"],
        "b1_cols": columns(a["L0_gnn_b1"]),
        "w2": a["L0_gnn_w2"],
        "b2": a["L0_gnn_b2"],
        "ln_gamma": a["L0_gnn_ln_gamma"],
        "ln_beta": a["L0_gnn_ln_beta"],
        "wq_t": np.ascontiguousarray(a["L1_gnn_Wq"].T),
        "bq_cols": columns(a["L1_gnn_bq"]),
        "wk_t": np.ascontiguousarray(a["L1_gnn_Wk"].T),
        "bk_cols": columns(a["L1_gnn_bk"]),
        "wv_t": np.ascontiguousarray(a["L1_gnn_Wv"].T),
        "bv": a["L1_gnn_bv"],
        "wo_t": np.ascontiguousarray(a["L1_gnn_Wo"].T),
        "bo": a["L1_gnn_bo"],
        "identity": np.eye(128, dtype=np.float32),
    }
    nc = bacc.Bacc("TRN2", target_bir_lowering=False, num_devices=1)
    args = [nc.dram_tensor(k, v.shape, mb.dt.from_np(v.dtype), kind="ExternalInput").ap() for k, v in arrays.items()]
    out = nc.dram_tensor("out", (B, n, f), mb.dt.float32, kind="ExternalOutput").ap()
    gat_then_attention_kernel(nc, *args, out)
    r = run_bass_kernel_spmd(nc, [arrays], core_ids=[0])
    return r.results[0]["out"]
```

```python
import concourse.bass as bass
from concourse import mybir
from contextlib import ExitStack


def gat_then_attention_kernel(nc: bass.Bass, x_t, x, adj, w_heads, a_heads, w_out, a_out, w1, b1_cols, w2, b2,
                              ln_gamma, ln_beta, wq_t, bq_cols, wk_t, bk_cols, wv_t, bv, wo_t, bo, identity, out):
    fp32 = mybir.dt.float32
    fp32r = mybir.dt.float32r
    bf16 = mybir.dt.bfloat16
    i32 = mybir.dt.int32
    ALU = mybir.AluOpType
    ACT = mybir.ActivationFunctionType
    AX = mybir.AxisListType

    N = 128
    F = x.shape[2]
    KT = F // 128
    PAIRS = x.shape[0] // 2
    GH = w_heads.shape[0]
    HF = GH * F
    HT = HF // 128
    AH = 8
    D = F // AH
    SCALE = float(D) ** -0.5
    LEAKY = 0.01
    EPS = 1e-5
    MASKED = -1e30
    NF = 2 * GH
    WC = NF + HF
    CH = 3
    CW = WC // CH
    assert CW * CH == WC and CW <= 512
    F2 = F + 2

    ctx = ExitStack()
    with ctx:
        def sb(name, shape, dt=fp32):
            return ctx.enter_context(nc.sbuf_tensor(name, shape, dt))

        def ps(name, shape):
            return ctx.enter_context(nc.psum_tensor(name, shape, fp32))

        def sem(name):
            return ctx.enter_context(nc.semaphore(name))

        ident = sb("ident", [128, 128])
        ident_bf = sb("ident_bf", [128, 128], bf16)
        adj_i = sb("adj_i", [128, N], i32)
        adj_f = sb("adj_f", [128, N])
        gat_mask = sb("gat_mask", [128, N], bf16)
        mha_mask = sb("mha_mask", [128, N], bf16)
        row_ok = sb("row_ok", [128, 3])
        ao_rows = sb("ao_rows", [128, 2 * F])
        small_names = ("w1", "w2", "wq", "wk", "wv", "wo")
        w_hi, w_lo = sb("w_hi", [128, KT, WC], fp32r), sb("w_lo", [128, KT, WC], fp32r)
        wout_hi, wout_lo = sb("wout_hi", [128, HT, F2], fp32r), sb("wout_lo", [128, HT, F2], fp32r)
        small = {k: (sb(k + "_hi", [128, KT, F], fp32r), sb(k + "_lo", [128, KT, F], fp32r)) for k in small_names}
        b1c, bqc, bkc = sb("b1c", [128, KT]), sb("bqc", [128, KT]), sb("bkc", [128, KT])
        b2r, gamr, betr, bvr, bor = (sb(n, [128, F]) for n in ("b2r", "gamr", "betr", "bvr", "bor"))
        neg_half = sb("neg_half", [128, 2])

        xt = sb("xt", [128, KT, 2, N])
        xt_hi, xt_lo = sb("xt_hi", [128, KT, 2, N], fp32r), sb("xt_lo", [128, KT, 2, N], fp32r)
        wh = [sb(f"wh{g}", [128, WC]) for g in range(2)]
        gat_probs = sb("gat_probs", [128, 3 * 2 * GH * N])
        t1, e1, p1 = ([gat_probs[:, (2 * i + g) * GH * N:(2 * i + g + 1) * GH * N].rearrange("p (h m) -> p h m", m=N)
                       for g in range(2)] for i in range(3))
        pt1 = [sb(f"pt1_{g}", [128, GH, N]) for g in range(2)]
        mx1 = [sb(f"mx1_{g}", [128, GH]) for g in range(2)]
        m1 = [sb(f"m1_{g}", [128, GH]) for g in range(2)]
        sum1 = [sb(f"sum1_{g}", [128, GH]) for g in range(2)]
        r1 = [sb(f"r1_{g}", [128, GH]) for g in range(2)]
        elu_in = sb("elu_in", [128, max(2 * HT * N, KT * WC)])
        em = [elu_in[:, g * HT * N:(g + 1) * HT * N].rearrange("p (t n) -> p t n", n=N) for g in range(2)]
        ht_hi = [sb(f"ht_hi{g}", [128, HT, N], fp32r) for g in range(2)]
        ht_lo = [sb(f"ht_lo{g}", [128, HT, N], fp32r) for g in range(2)]
        wh2 = sb("wh2", [128, 2, F2])

        xn = sb("xn", [128, 2, F])
        xb = sb("xb", [128, 2, F])
        t2, e2, p2, pt2 = (sb(n, [128, 2, N]) for n in ("t2", "e2", "p2", "pt2"))
        mx2, m2, sum2, r2 = (sb(n, [128, 2]) for n in ("mx2", "m2", "sum2", "r2"))
        em2, gat = sb("em2", [128, 2, F]), sb("gat", [128, 2, F])
        row_bufs = sb("row_bufs", [128, 6 * 2 * F])
        gat_b2, y1, z1, x1, x1b, v = (row_bufs[:, i * 2 * F:(i + 1) * 2 * F].rearrange("p (g f) -> p g f", g=2)
                                      for i in range(6))
        gt_hi, gt_lo = sb("gt_hi", [128, KT, 2, N], fp32r), sb("gt_lo", [128, KT, 2, N], fp32r)
        hid = sb("hid", [128, KT, 2, N])
        hid_hi, hid_lo = sb("hid_hi", [128, KT, 2, N], fp32r), sb("hid_lo", [128, KT, 2, N], fp32r)
        stats = [sb(f"stats{i}", [128, 2, 6]) for i in range(3)]
        mv = [sb(f"mv{i}", [128, 2, 2]) for i in range(3)]
        ve = [sb(f"ve{i}", [128, 2]) for i in range(3)]
        rstd = [sb(f"rstd{i}", [128, 2]) for i in range(3)]
        x1t_hi, x1t_lo = sb("x1t_hi", [128, KT, 2, N], fp32r), sb("x1t_lo", [128, KT, 2, N], fp32r)
        qt, kt = sb("qt", [128, KT, 2, N]), sb("kt", [128, KT, 2, N])
        mx3 = [sb(f"mx3_{g}", [128, AH]) for g in range(2)]
        nb3 = [sb(f"nb3_{g}", [128, AH]) for g in range(2)]
        sum3 = [sb(f"sum3_{g}", [128, AH]) for g in range(2)]
        r3 = [sb(f"r3_{g}", [128, AH]) for g in range(2)]
        mha_probs = sb("mha_probs", [128, max(6 * AH * N, 4 * AH * N + HT * F2)])
        e3, p3, pt3 = ([mha_probs[:, (2 * i + g) * AH * N:(2 * i + g + 1) * AH * N].rearrange("p (h m) -> p h m", m=N)
                        for g in range(2)] for i in range(3))
        at_hi, at_lo = sb("at_hi", [128, KT, 2, N], fp32r), sb("at_lo", [128, KT, 2, N], fp32r)
        y3, fin = sb("y3", [128, 2, F]), sb("fin", [128, 2, F])

        small_in = {k: row_bufs[:, i * KT * F:(i + 1) * KT * F].rearrange("p (t o) -> p t o", t=KT)
                    for i, k in enumerate(small_names)}
        w_in = elu_in[:, 0:KT * WC].rearrange("p (t c) -> p t c", t=KT)
        a_rows = mha_probs[:, 0:2 * GH * F].rearrange("p (h j) -> p h j", h=GH)
        prod = mha_probs[:, 2 * GH * F:2 * GH * F + HT * F].rearrange("p (t o) -> p t o", t=HT)
        wout_in = mha_probs[:, 4 * GH * F:4 * GH * F + HT * F2].rearrange("p (t c) -> p t c", t=HT)

        tri = ps("tri", [128, 3, 512])
        mid = ps("mid", [128, 512])
        wide_b = ps("wide_b", [128, 2, 512])
        wide_a = ps("wide_a", [128, 2, 512])
        wide = [wide_a, wide_b]

        def heads(bank):
            return bank.rearrange("p (h m) -> p h m", m=N)

        s1_ps = pt1_ps = heads(mid[:, :])
        s2_ps = pt2_ps = heads(mid[:, 0:2 * N])
        wh2_ps = [mid[:, 0:F2], tri[:, 1, 0:F2]]
        gat_ps = wide_a[:, 0, :].rearrange("p (g f) -> p g f", g=2)
        gt_ps = wide_a[:, 1, :].rearrange("p (t g n) -> p t g n", t=KT, g=2)
        pt3_ps = [wide_b[:, :, :], tri[:, 0:2, :]]
        tri_t = [tri[:, c, :].rearrange("p (t g n) -> p t g n", t=KT, g=2) for c in range(3)]
        tri_g = [tri[:, c, :].rearrange("p (g f) -> p g f", g=2) for c in range(3)]
        at_ps, x1t_ps, v_ps = tri_t[0], tri_t[0], tri_g[0]
        y1_ps, q_ps = tri_g[1], tri_t[1]
        hid_ps, y3_ps, k_ps = tri_t[2], tri_g[2], tri_t[2]

        s_adj, s_win, s_wout, s_small, s_rows, s_cols = (
            sem("load_" + n) for n in ("adj", "w_in", "w_out", "small", "rows", "cols"))
        s_idn, s_const, s_masks, s_dsc, s_wready, s_smallw = (
            sem(n) for n in ("ident_loaded", "constants_ready", "masks_ready", "setup_chain", "weights_ready",
                             "small_weights_ready"))
        s_smallhi = sem("small_heads_ready")
        s_group = sem("score_row_group_done")
        s_passed = sem("waits_passed")
        s_xt, s_xn, s_store = sem("xt_loaded"), sem("xn_loaded"), sem("out_stored")
        s_xhi, s_xsplit = sem("xt_hi_ready"), sem("xt_split")
        s_whmm, s_wh = sem("wh_mm"), sem("wh_ready")
        s_s1, s_t1, s_mx1, s_lk1, s_m1, s_d1, s_e1 = (
            sem(n) for n in ("s1_mm", "t1_ready", "mx1_ready", "leaky1", "m1_ready", "d1_ready", "e1_ready"))
        s_sum1, s_r1, s_p1, s_pt1mm, s_pt1 = (sem(n) for n in ("sum1", "r1_ready", "p1_ready", "pt1_mm", "pt1_ready"))
        s_htmm, s_eh, s_em, s_h, s_hhi = (
            sem(n) for n in ("ht_mm", "eh_ready", "em_ready", "h_ready", "ht_hi_ready"))
        s_hlo, s_hlo1b = sem("ht_lo_ready"), sem("ht_lo_graph1_second_half_ready")
        s_wh2mm, s_wh2 = sem("wh2_mm"), sem("wh2_ready")
        s_xb = sem("xb_ready")
        s_s2, s_t2, s_mx2, s_lk2, s_m2, s_d2, s_e2, s_sum2, s_r2, s_p2, s_pt2mm, s_pt2 = (
            sem(n) for n in ("s2_mm", "t2_ready", "mx2_ready", "leaky2", "m2_ready", "d2_ready", "e2_ready", "sum2",
                             "r2_ready", "p2_ready", "pt2_mm", "pt2_ready"))
        s_gatmm, s_eo, s_em2, s_gat, s_gatb2, s_gtmm, s_gthi, s_gtlo = (
            sem(n) for n in ("gat_mm", "eo_ready", "em2_ready", "gat_ready", "gat_b2_ready", "gt_mm", "gt_hi_ready",
                             "gt_lo_ready"))
        s_hidmm, s_hid, s_hidhi, s_hidlo, s_y1mm, s_y1 = (
            sem(n) for n in ("hid_mm", "hid_ready", "hid_hi_ready", "hid_lo_ready", "y1_mm", "y1_ready"))
        s_st = [sem(f"stats{i}_ready") for i in range(3)]
        s_mv = [sem(f"mv{i}_ready") for i in range(3)]
        s_ve = [sem(f"var_eps{i}_ready") for i in range(3)]
        s_rstd = [sem(f"rstd{i}_ready") for i in range(3)]
        s_g1, s_z1, s_x1, s_x1b = (sem(n) for n in ("y1_gamma", "z1_ready", "x1_ready", "x1b_ready"))
        s_x1tmm, s_x1thi, s_x1tlo = sem("x1t_mm"), sem("x1t_hi_ready"), sem("x1t_lo_ready")
        s_qmm, s_kmm, s_vmm, s_qt, s_kt, s_v = (
            sem(n) for n in ("q_mm", "k_mm", "v_mm", "q_ready", "k_ready", "v_ready"))
        s_mx3, s_nb3, s_e3, s_ri3, s_r3, s_p3, s_pt3mm, s_pt3 = (
            sem(n) for n in ("mx3_ready", "nb3_ready", "e3_ready", "recip3", "r3_ready", "p3_ready",
                             "pt3_mm", "pt3_ready"))
        s_atmm, s_athi, s_atlo, s_y3mm, s_y3, s_fin = (
            sem(n) for n in ("at_mm", "at_hi_ready", "at_lo_ready", "y3_mm", "y3_ready", "fin_ready"))

        def wait(eng, semaphore, value):
            if not isinstance(value, int) or value > 0:
                eng.wait_ge(semaphore, value)

        def wait_apart(eng, semaphore, value):
            wait(eng, semaphore, value)
            eng.sem_inc(s_passed, 1)

        def per_head(column, n=N):
            return column.unsqueeze(2).to_broadcast([128, column.shape[1], n])

        def run_steps(eng, step):
            for s in range(3):
                step(s, True, s >= 1, s >= 2)
            with eng.Fori(3, PAIRS - 1) as s:
                step(s, True, True, True)
            step(PAIRS - 1, True, True, True)
            step(PAIRS, False, True, True)
            step(PAIRS + 1, False, False, True)

        block = ctx.enter_context(nc.Block())

        @block.sync
        def _(sp):
            def load_xt(p):
                wait(sp, s_xsplit, p)
                sp.dma_start(xt[:, :, :, :], x_t[p]).then_inc(s_xt, 16)

            sp.dma_start(adj_i[:, :], adj).then_inc(s_adj, 16)
            sp.dma_start(ident[:, :], identity).then_inc(s_idn, 16)
            load_xt(0)
            sp.dma_start(a_rows[:, :, :], a_heads.unsqueeze(0).to_broadcast([128, GH, 2 * F])).then_inc(s_win, 16)
            for k in range(KT):
                sp.dma_start(w_in[:, k, NF:].rearrange("p (h o) -> p h o", h=GH),
                             w_heads[:, k * 128:(k + 1) * 128, :].rearrange("h p o -> p h o")).then_inc(s_win, 16)
            sp.dma_start(ao_rows[:, :], a_out.unsqueeze(0).to_broadcast([128, 2 * F])).then_inc(s_wout, 16)
            sp.dma_start(wout_in[:, :, 0:F], w_out.rearrange("(t p) o -> p t o", p=128)).then_inc(s_wout, 16)
            for name, w in (("w1", w1), ("w2", w2), ("wq", wq_t), ("wk", wk_t), ("wv", wv_t), ("wo", wo_t)):
                sp.dma_start(small_in[name][:, :, :], w.rearrange("(t p) o -> p t o", p=128)).then_inc(s_small, 16)
            for dst, src in ((b1c, b1_cols), (bqc, bq_cols), (bkc, bk_cols)):
                sp.dma_start(dst[:, :], src).then_inc(s_cols, 16)
            for dst, src in ((b2r, b2), (gamr, ln_gamma), (betr, ln_beta), (bvr, bv), (bor, bo)):
                sp.dma_start(dst[:, :], src.unsqueeze(0).to_broadcast([128, F])).then_inc(s_rows, 16)

            def step(s, front, middle, end):
                if front:
                    if not isinstance(s, int) or s + 1 < PAIRS:
                        load_xt(s + 1)
                    wait(sp, s_xb, s)
                    sp.dma_start(xn[:, :, :], x[bass.ds(2 * s, 2)].rearrange("g n f -> n g f")).then_inc(s_xn, 16)
                if end:
                    sp.wait_ge(s_fin, 2 * s - 2)
                    sp.dma_start(out[bass.ds(2 * s - 4, 2)].rearrange("g n f -> n g f"), fin[:, :, :]).then_inc(s_store, 16)

            run_steps(sp, step)
            sp.wait_ge(s_store, 16 * PAIRS)

        @block.tensor
        def _(pe):
            def split_mm(dst, hi_l, lo_l, hi_r, lo_r, first, last):
                nc.tensor.matmul(dst, lo_l, hi_r, start=first, stop=False)
                nc.tensor.matmul(dst, hi_l, lo_r, start=False, stop=False)
                return nc.tensor.matmul(dst, hi_l, hi_r, start=False, stop=last)

            def first_features(p, g, c):
                if g == 0 and c == 0:
                    pe.wait_ge(s_xsplit, p + 1)
                    wait(pe, s_v, p - 1)
                if g == 0 and c == 1:
                    wait(pe, s_qt, 2 * (p - 1))
                if g == 0 and c == 2:
                    wait(pe, s_kt, 2 * (p - 1))
                if g == 1:
                    pe.wait_ge(s_wh, 6 * p + c + 1)
                for k in range(KT):
                    cols = slice(c * CW, (c + 1) * CW)
                    last = split_mm(tri[:, c, 0:CW], xt_hi[:, k, g, :], xt_lo[:, k, g, :], w_hi[:, k, cols],
                                    w_lo[:, k, cols], k == 0, k == KT - 1)
                last.then_inc(s_whmm, 1)

            def gat_scores1(p, g):
                pe.wait_ge(s_wh, 6 * p + 3 * g + 1)
                if g == 0:
                    wait(pe, s_pt2, p)
                else:
                    pe.wait_ge(s_t1, 2 * p + 1)
                nc.tensor.matmul(s1_ps, ident_bf[:, :], gat_mask[:, :].unsqueeze(1).to_broadcast([128, GH, N]),
                                 start=True, stop=False)
                for h in range(GH):
                    last = nc.tensor.matmul(s1_ps[:, h, :], wh[g][:, GH + h:GH + h + 1].to_broadcast([128, 128]),
                                            ident[:, :], is_transpose=True, start=False, stop=(h == GH - 1))
                last.then_inc(s_s1, 1)

            def transpose_p1(p, g):
                pe.wait_ge(s_p1, 2 * p + g + 1)
                if g == 0:
                    pe.wait_ge(s_t1, 2 * p + 2)
                else:
                    pe.wait_ge(s_pt1, 2 * p + 1)
                for h in range(GH):
                    last = nc.tensor.transpose(pt1_ps[:, h, :], p1[g][:, h, :], ident[:, :])
                last.then_inc(s_pt1mm, 1)

            def gat_values1(p, g):
                pe.wait_ge(s_pt1, 2 * p + g + 1)
                pe.wait_ge(s_wh, 6 * p + 3 * g + 3)
                if g == 0:
                    wait(pe, s_gtlo, p)
                else:
                    wait(pe, s_pt3, 4 * (p - 2) + 2)
                for t in range(HT):
                    dst = wide[g][:, t // 4, (t % 4) * N:(t % 4 + 1) * N]
                    last = nc.tensor.matmul(dst, wh[g][:, NF + t * 128:NF + (t + 1) * 128], pt1[g][:, t // KT, :],
                                            start=True, stop=True)
                    if t % 4 == 3:
                        last.then_inc(s_htmm, 1)

            def second_features(p, g, half):
                pe.wait_ge(s_hhi, 4 * p + 2 * g + half + 1)
                if half == 0 and g == 0:
                    pe.wait_ge(s_pt1, 2 * p + 2)
                if half == 0 and g == 1:
                    wait(pe, s_y1, p)
                tiles = range(4 * half, 4 * half + 4)
                for t in tiles:
                    nc.tensor.matmul(wh2_ps[g], ht_hi[g][:, t, :], wout_lo[:, t, :], start=(t == 0), stop=False)
                    nc.tensor.matmul(wh2_ps[g], ht_hi[g][:, t, :], wout_hi[:, t, :], start=False, stop=False)
                if g == 1 and half == 1:
                    pe.wait_ge(s_hlo1b, p + 1)
                else:
                    pe.wait_ge(s_hlo, 3 * p + 2 * g + half + 1)
                for t in tiles:
                    last = nc.tensor.matmul(wh2_ps[g], ht_lo[g][:, t, :], wout_hi[:, t, :], start=False,
                                            stop=(t == HT - 1))
                if half == 1:
                    last.then_inc(s_wh2mm, 1)

            def gat_scores2(p):
                pe.wait_ge(s_wh2, 2 * p + 2)
                nc.tensor.matmul(s2_ps, ident_bf[:, :], gat_mask[:, :].unsqueeze(1).to_broadcast([128, 2, N]),
                                 start=True, stop=False)
                for g in range(2):
                    last = nc.tensor.matmul(s2_ps[:, g, :], wh2[:, g, F + 1:F + 2].to_broadcast([128, 128]),
                                            ident[:, :], is_transpose=True, start=False, stop=(g == 1))
                last.then_inc(s_s2, 1)

            def transpose_p2(q):
                pe.wait_ge(s_p2, q + 1)
                for g in range(2):
                    last = nc.tensor.transpose(pt2_ps[:, g, :], p2[:, g, :], ident[:, :])
                last.then_inc(s_pt2mm, 1)

            def gat_values2(q):
                pe.wait_ge(s_pt2, q + 1)
                wait(pe, s_e3, AH * (2 * q - 1))
                for g in range(2):
                    last = nc.tensor.matmul(gat_ps[:, g, :], pt2[:, g, :], wh2[:, g, 0:F], start=True, stop=True)
                last.then_inc(s_gatmm, 1)

            def transpose_gat(q):
                pe.wait_ge(s_gat, q + 1)
                for t in range(KT):
                    for g in range(2):
                        last = nc.tensor.transpose(gt_ps[:, t, g, :], gat[:, g, t * 128:(t + 1) * 128], ident[:, :])
                last.then_inc(s_gtmm, 1)

            def transposed_product(dst, weight, hi, lo, lo_ready, count):
                w_h, w_l = small[weight]
                for m in range(KT):
                    cols = slice(m * 128, (m + 1) * 128)
                    for k in range(KT):
                        nc.tensor.matmul(dst[:, m, :, :], w_l[:, k, cols], hi[:, k, :, :], start=(k == 0), stop=False)
                        nc.tensor.matmul(dst[:, m, :, :], w_h[:, k, cols], hi[:, k, :, :], start=False, stop=False)
                    if m == 0:
                        pe.wait_ge(lo_ready, count)
                    for k in range(KT):
                        last = nc.tensor.matmul(dst[:, m, :, :], w_h[:, k, cols], lo[:, k, :, :], start=False,
                                                stop=(k == KT - 1))
                return last

            def natural_product(dst, weight, hi, lo, lo_ready, count):
                w_h, w_l = small[weight]
                for g in range(2):
                    for k in range(KT):
                        nc.tensor.matmul(dst[:, g, :], hi[:, k, g, :], w_l[:, k, :], start=(k == 0), stop=False)
                        nc.tensor.matmul(dst[:, g, :], hi[:, k, g, :], w_h[:, k, :], start=False, stop=False)
                    if g == 0:
                        pe.wait_ge(lo_ready, count)
                    for k in range(KT):
                        last = nc.tensor.matmul(dst[:, g, :], lo[:, k, g, :], w_h[:, k, :], start=False,
                                                stop=(k == KT - 1))
                return last

            def ffn_up(q, front):
                pe.wait_ge(s_gthi, q + 1)
                if front:
                    pe.wait_ge(s_wh, 6 * q + 12)
                transposed_product(hid_ps, "w1", gt_hi, gt_lo, s_gtlo, q + 1).then_inc(s_hidmm, 1)

            def ffn_down(q):
                pe.wait_ge(s_hidhi, 2 * q + 2)
                wait(pe, s_pt3, 4 * q)
                natural_product(y1_ps, "w2", hid_hi, hid_lo, s_hidlo, q + 1).then_inc(s_y1mm, 1)

            def transpose_x1(q):
                pe.wait_ge(s_x1, 2 * q + 2)
                wait(pe, s_atlo, q)
                for t in range(KT):
                    for g in range(2):
                        last = nc.tensor.transpose(x1t_ps[:, t, g, :], x1[:, g, t * 128:(t + 1) * 128], ident[:, :])
                last.then_inc(s_x1tmm, 1)

            def keys(q):
                pe.wait_ge(s_x1thi, q + 1)
                wait(pe, s_y3, q)
                transposed_product(k_ps, "wk", x1t_hi, x1t_lo, s_x1tlo, q + 1).then_inc(s_kmm, 1)

            def queries(q, front):
                if front:
                    pe.wait_ge(s_wh2, 2 * q + 4)
                transposed_product(q_ps, "wq", x1t_hi, x1t_lo, s_x1tlo, q + 1).then_inc(s_qmm, 1)

            def values3(q):
                natural_product(v_ps, "wv", x1t_hi, x1t_lo, s_x1tlo, q + 1).then_inc(s_vmm, 1)

            def mha_scores(q, g, front):
                pe.wait_ge(s_qt, 2 * q + 2)
                pe.wait_ge(s_kt, 2 * q + 2)
                if front:
                    pe.wait_ge(s_h, 4 * (q + 1) + 2 * g + 2)
                elif g == 1:
                    pe.wait_ge(s_pt3, 4 * (q - 1) + 2)
                else:
                    pe.wait_ge(s_gtlo, q + 1)
                for b in range(2):
                    nc.tensor.matmul(heads(wide[g][:, b, :]), ident_bf[:, :],
                                     mha_mask[:, :].unsqueeze(1).to_broadcast([128, 4, N]), start=True, stop=False,
                                     skip_group_check=True)
                for r in range(4):
                    rows = slice(32 * r, 32 * r + 32)
                    if r >= 2:
                        pe.wait_ge(s_group, 8 * q + 4 * g + r - 1)
                    for t in range(KT):
                        b, c = head_place(r, t)
                        last = nc.tensor.matmul(wide[g][:, b, c * N:(c + 1) * N], qt[rows, t, g, :], kt[rows, t, g, :],
                                                start=False, stop=(r >= 2 and t == KT - 1), skip_group_check=True)
                    last.then_inc(s_group, 1)

            def transpose_p3(z, g, front):
                if g == 0:
                    pe.wait_ge(s_e3, AH * (2 * z + 2))
                for b in range(2):
                    if g == 1 and front:
                        pe.wait_ge(s_wh, 6 * (z + 2) + 4 + b)
                    if g == 1 and not front and b == 0:
                        pe.wait_ge(s_v, z + 1)
                    pe.wait_ge(s_p3, 4 * z + 2 * g + b + 1)
                    for c in range(4):
                        last = nc.tensor.transpose(pt3_ps[g][:, b, c * N:(c + 1) * N], p3[g][:, 4 * b + c, :],
                                                   ident[:, :])
                    last.then_inc(s_pt3mm, 1)

            def mha_values(z):
                pe.wait_ge(s_v, z + 1)
                pe.wait_ge(s_pt3, 4 * z + 4)
                for g in range(2):
                    for t in range(KT):
                        for r in range(4):
                            b, c = head_place(r, t)
                            head = 4 * t + r
                            last = nc.tensor.matmul(at_ps[32 * r:32 * r + 32, t, g, :], v[:, g, head * D:(head + 1) * D],
                                                    pt3[g][:, 4 * b + c, :], start=True, stop=True)
                last.then_inc(s_atmm, 1)

            def out_projection(q, middle):
                if middle:
                    pe.wait_ge(s_hidhi, 2 * q + 4)
                pe.wait_ge(s_athi, q + 1)
                natural_product(y3_ps, "wo", at_hi, at_lo, s_atlo, q + 1).then_inc(s_y3mm, 1)

            def head_place(r, t):
                return r % 2, 2 * (r // 2) + t

            pe.wait_ge(s_idn, 16)
            pe.wait_ge(s_masks, 3)
            pe.wait_ge(s_wready, 1)

            def step(s, front, middle, end):
                q, z = s - 1, s - 2
                if front:
                    first_features(s, 0, 0)
                if middle:
                    transpose_p2(q)
                if front:
                    first_features(s, 0, 1)
                    first_features(s, 0, 2)
                    gat_scores1(s, 0)
                if middle:
                    gat_values2(q)
                if front:
                    first_features(s, 1, 0)
                    first_features(s, 1, 1)
                if front:
                    first_features(s, 1, 2)
                    gat_scores1(s, 1)
                if middle:
                    transpose_gat(q)
                if end:
                    transpose_p3(z, 0, front)
                    transpose_p3(z, 1, front)
                if front:
                    transpose_p1(s, 0)
                if middle:
                    if isinstance(s, int) and s == 1:
                        pe.wait_ge(s_smallw, len(small))
                    ffn_up(q, front)
                if front:
                    gat_values1(s, 0)
                if end:
                    mha_values(z)
                if front:
                    transpose_p1(s, 1)
                if middle:
                    ffn_down(q)
                if front:
                    gat_values1(s, 1)
                if end:
                    out_projection(z, middle)
                if front:
                    if isinstance(s, int) and s == 0:
                        pe.wait_ge(s_wready, 2)
                    second_features(s, 0, 0)
                    second_features(s, 0, 1)
                    second_features(s, 1, 0)
                if middle:
                    transpose_x1(q)
                if front:
                    second_features(s, 1, 1)
                if middle:
                    keys(q)
                    queries(q, front)
                if front:
                    gat_scores2(s)
                if middle:
                    values3(q)
                    mha_scores(q, 0, front)
                    mha_scores(q, 1, front)

            run_steps(pe, step)

        @block.scalar
        def _(act):
            def wh_out(p, g, c):
                act.wait_ge(s_whmm, 6 * p + 3 * g + c + 1)
                wait(act, s_htmm, 4 * (p - 1) + 2 * g + 2)
                nc.scalar.activation(wh[g][:, c * CW:(c + 1) * CW], tri[:, c, 0:CW], ACT.Copy).then_inc(s_wh, 1)

            def exp1(p, g):
                act.wait_ge(s_d1, 2 * p + g + 1)
                nc.scalar.activation(e1[g][:, :, :], e1[g][:, :, :], ACT.Exp).then_inc(s_e1, 1)

            def pt1_out(p, g):
                act.wait_ge(s_pt1mm, 2 * p + g + 1)
                nc.scalar.activation(pt1[g][:, :, :], pt1_ps, ACT.Copy).then_inc(s_pt1, 1)

            def exp_values1(p, g):
                wait(act, s_hlo, 3 * (p - 1) + 2 + g)
                if g == 1:
                    wait(act, s_hlo1b, p)
                for b in range(2):
                    act.wait_ge(s_htmm, 4 * p + 2 * g + b + 1)
                    nc.scalar.activation(em[g][:, 4 * b:4 * b + 4, :], heads(wide[g][:, b, :]), ACT.Relu,
                                         scale=-1.0).then_inc(s_em, 1)
                for b in range(2):
                    act.wait_ge(s_em, 4 * p + 2 * g + b + 1)
                    nc.scalar.activation(em[g][:, 4 * b:4 * b + 4, :], em[g][:, 4 * b:4 * b + 4, :], ACT.Exp,
                                         scale=-1.0).then_inc(s_eh, 1)

            def values1_head(p, g):
                wait(act, s_wh2mm, 2 * (p - 1) + g + 1)
                for b in range(2):
                    act.wait_ge(s_h, 4 * p + 2 * g + b + 1)
                    nc.scalar.activation(ht_hi[g][:, 4 * b:4 * b + 4, :], em[g][:, 4 * b:4 * b + 4, :],
                                         ACT.Copy).then_inc(s_hhi, 1)

            def wh2_out(p, g):
                act.wait_ge(s_wh2mm, 2 * p + g + 1)
                nc.scalar.activation(wh2[:, g, :], wh2_ps[g], ACT.Copy).then_inc(s_wh2, 1)

            def exp2(q):
                act.wait_ge(s_d2, q + 1)
                nc.scalar.activation(e2[:, :, :], e2[:, :, :], ACT.Exp).then_inc(s_e2, 1)

            def pt2_out(q):
                act.wait_ge(s_pt2mm, q + 1)
                nc.scalar.activation(pt2[:, :, :], pt2_ps, ACT.Copy).then_inc(s_pt2, 1)

            def exp_gat(q):
                act.wait_ge(s_gatmm, q + 1)
                nc.scalar.activation(em2[:, :, :], gat_ps, ACT.Relu, scale=-1.0).then_inc(s_em2, 1)
                act.wait_ge(s_em2, q + 1)
                nc.scalar.activation(em2[:, :, :], em2[:, :, :], ACT.Exp, scale=-1.0).then_inc(s_eo, 1)

            def gt_hi_out(q):
                act.wait_ge(s_gtmm, q + 1)
                nc.scalar.activation(gt_hi[:, :, :, :], gt_ps, ACT.Copy).then_inc(s_gthi, 1)

            def hidden_out(q):
                act.wait_ge(s_hidmm, q + 1)
                for dst, done in ((hid, s_hid), (hid_hi, s_hidhi)):
                    for t in range(KT):
                        nc.scalar.activation(dst[:, t, :, :], hid_ps[:, t, :, :], ACT.Relu,
                                             bias=b1c[:, t:t + 1]).then_inc(done, 1)

            def x1t_hi_out(q):
                act.wait_ge(s_x1tmm, q + 1)
                nc.scalar.activation(x1t_hi[:, :, :, :], x1t_ps, ACT.Copy).then_inc(s_x1thi, 1)

            def qk_out(q):
                for mm, src, bias, dst, done in ((s_kmm, k_ps, bkc, kt, s_kt), (s_qmm, q_ps, bqc, qt, s_qt)):
                    act.wait_ge(mm, q + 1)
                    for t in range(KT):
                        nc.scalar.activation(dst[:, t, :, :], src[:, t, :, :], ACT.Identity,
                                             bias=bias[:, t:t + 1]).then_inc(done, 1)

            def exp3(q, g, half):
                act.wait_ge(s_nb3, 2 * q + g + 1)
                for i in range(4 * half, 4 * half + 4):
                    nc.scalar.activation(e3[g][:, i, :], wide[g][:, half, (i % 4) * N:(i % 4 + 1) * N], ACT.Exp,
                                         scale=SCALE, bias=nb3[g][:, i:i + 1],
                                         accum_out=sum3[g][:, i:i + 1]).then_inc(s_e3, 1)

            def pt3_out(z, g):
                for b in range(2):
                    act.wait_ge(s_pt3mm, 4 * z + 2 * g + b + 1)
                    nc.scalar.activation(pt3[g][:, 4 * b:4 * b + 4, :], heads(pt3_ps[g][:, b, :]), ACT.Copy).then_inc(s_pt3, 1)

            def at_hi_out(q):
                act.wait_ge(s_atmm, q + 1)
                nc.scalar.activation(at_hi[:, :, :, :], at_ps, ACT.Copy).then_inc(s_athi, 1)

            def small_heads():
                act.wait_ge(s_small, 16 * len(small))
                for name, (hi, _) in small.items():
                    nc.scalar.activation(hi[:, :, :], small_in[name], ACT.Copy).then_inc(s_smallhi, 1)
                act.wait_ge(s_cols, 48)

            small_heads()

            def step(s, front, middle, end):
                q, z = s - 1, s - 2
                if middle:
                    pt2_out(q)
                if front:
                    wh_out(s, 0, 0)
                if end:
                    exp3(z, 1, 0)
                if front:
                    wh_out(s, 0, 1)
                    wh_out(s, 0, 2)
                if middle:
                    exp_gat(q)
                if front:
                    wh_out(s, 1, 0)
                if end:
                    exp3(z, 1, 1)
                if front:
                    exp1(s, 0)
                    wh_out(s, 1, 1)
                    wh_out(s, 1, 2)
                if middle:
                    gt_hi_out(q)
                if end:
                    pt3_out(z, 0)
                    pt3_out(z, 1)
                if front:
                    pt1_out(s, 0)
                    exp1(s, 1)
                if middle:
                    hidden_out(q)
                if front:
                    exp_values1(s, 0)
                if front:
                    pt1_out(s, 1)
                if end:
                    at_hi_out(z)
                if front:
                    values1_head(s, 0)
                    exp_values1(s, 1)
                    values1_head(s, 1)
                    wh2_out(s, 0)
                if middle:
                    x1t_hi_out(q)
                if front:
                    wh2_out(s, 1)
                if middle:
                    qk_out(q)
                if front:
                    exp2(s)
                if middle:
                    exp3(q, 0, 0)
                    exp3(q, 0, 1)

            run_steps(act, step)

        @block.vector
        def _(dve):
            V = nc.vector
            chain = [0]

            def link(ins):
                chain[0] += 1
                ins.then_inc(s_dsc, 1)
                dve.wait_ge(s_dsc, chain[0])

            def split(src, hi, lo, done):
                link(V.tensor_copy(hi, src))
                V.tensor_tensor(lo, src, hi.bitcast(fp32), ALU.subtract).then_inc(done, 1)

            def split_xt(p):
                dve.wait_ge(s_xt, 16 * (p + 1))
                wait(dve, s_whmm, 6 * p)
                V.tensor_copy(xt_hi[:, :, :, :], xt[:, :, :, :]).then_inc(s_xhi, 1)
                dve.wait_ge(s_xhi, p + 1)
                V.tensor_tensor(xt_lo[:, :, :, :], xt[:, :, :, :], xt_hi[:, :, :, :].bitcast(fp32),
                                ALU.subtract).then_inc(s_xsplit, 1)

            def leaky(dst, src, done):
                V.scalar_tensor_tensor(out=dst, in0=src, scalar=LEAKY, in1=src, op0=ALU.mult,
                                       op1=ALU.max).then_inc(done, 1)

            def scores1(p, g):
                dve.wait_ge(s_s1, 2 * p + g + 1)
                V.tensor_tensor(t1[g][:, :, :], s1_ps, per_head(wh[g][:, 0:GH]), ALU.add).then_inc(s_t1, 1)

            def leaky_scores1(p, g):
                dve.wait_ge(s_t1, 2 * p + g + 1)
                V.reduce_max(mx1[g][:, :], t1[g][:, :, :], AX.X).then_inc(s_mx1, 1)
                wait(dve, s_p1, 2 * (p - 1) + g + 1)
                leaky(e1[g][:, :, :], t1[g][:, :, :], s_lk1)
                dve.wait_ge(s_mx1, 2 * p + g + 1)
                leaky(m1[g][:, :], mx1[g][:, :], s_m1)

            def sums1(p, g):
                dve.wait_ge(s_e1, 2 * p + g + 1)
                V.reduce_sum(sum1[g][:, :], e1[g][:, :, :], AX.X).then_inc(s_sum1, 1)
                dve.wait_ge(s_sum1, 2 * p + g + 1)
                wait(dve, s_p1, 2 * (p - 1) + g + 1)
                V.reciprocal(r1[g][:, :], sum1[g][:, :]).then_inc(s_r1, 1)

            def elu1(p, g, b):
                part = em[g][:, 4 * b:4 * b + 4, :]
                dve.wait_ge(s_eh, 4 * p + 2 * g + b + 1)
                V.scalar_tensor_tensor(out=part, in0=part, scalar=-1.0, in1=heads(wide[g][:, b, :]), op0=ALU.add,
                                       op1=ALU.max).then_inc(s_h, 1)

            def elu1_last_tail(p):
                dve.wait_ge(s_hhi, 4 * p + 4)
                V.tensor_tensor(ht_lo[1][:, 4:8, :], em[1][:, 4:8, :], ht_hi[1][:, 4:8, :].bitcast(fp32),
                                ALU.subtract).then_inc(s_hlo1b, 1)

            def scores2(q):
                dve.wait_ge(s_s2, q + 1)
                V.tensor_tensor(t2[:, :, :], s2_ps, wh2[:, :, F:F + 1].to_broadcast([128, 2, N]), ALU.add).then_inc(s_t2, 1)
                dve.wait_ge(s_t2, q + 1)
                V.reduce_max(mx2[:, :], t2[:, :, :], AX.X).then_inc(s_mx2, 1)
                leaky(e2[:, :, :], t2[:, :, :], s_lk2)
                dve.wait_ge(s_mx2, q + 1)
                leaky(m2[:, :], mx2[:, :], s_m2)

            def less_max2(q):
                dve.wait_ge(s_lk2, q + 1)
                dve.wait_ge(s_m2, q + 1)
                V.tensor_tensor(e2[:, :, :], e2[:, :, :], per_head(m2[:, :]), ALU.subtract).then_inc(s_d2, 1)

            def sums2(q):
                dve.wait_ge(s_e2, q + 1)
                V.reduce_sum(sum2[:, :], e2[:, :, :], AX.X).then_inc(s_sum2, 1)
                dve.wait_ge(s_sum2, q + 1)
                V.reciprocal(r2[:, :], sum2[:, :]).then_inc(s_r2, 1)

            def elu2(q):
                dve.wait_ge(s_eo, q + 1)
                V.scalar_tensor_tensor(out=gat[:, :, :], in0=em2[:, :, :], scalar=-1.0, in1=gat_ps, op0=ALU.add,
                                       op1=ALU.max).then_inc(s_gat, 1)

            def tail_out(q, head_ready, src, hi, lo, done):
                dve.wait_ge(head_ready, q + 1)
                V.tensor_tensor(lo[:, :, :, :], src, hi[:, :, :, :].bitcast(fp32), ALU.subtract).then_inc(done, 1)

            def hidden_tail(q):
                dve.wait_ge(s_hidhi, 2 * q + 2)
                V.tensor_tensor(hid_lo[:, :, :, :], hid[:, :, :, :], hid_hi[:, :, :, :].bitcast(fp32),
                                ALU.subtract).then_inc(s_hidlo, 1)

            def norm_stats(i, q, src, ready, count):
                for g in range(2):
                    dve.wait_ge(ready, count * q + (g + 1 if count == 2 else 1))
                    V.bn_stats(stats[i][:, g, :], src[:, g, :]).then_inc(s_st[i], 1)
                wait_apart(dve, s_st[i], 2 * q + 2)
                for g in range(2):
                    V.bn_aggr(mv[i][:, g, :], stats[i][:, g, :]).then_inc(s_mv[i], 1)
                dve.wait_ge(s_mv[i], 2 * q + 2)
                V.tensor_scalar(ve[i][:, :], mv[i][:, :, 1], EPS, None, ALU.add).then_inc(s_ve[i], 1)

            def gat_sum(q):
                dve.wait_ge(s_y1mm, q + 1)
                dve.wait_ge(s_gatb2, q + 1)
                V.tensor_tensor(y1, y1_ps, gat_b2, ALU.add).then_inc(s_y1, 1)

            def gat_gamma(q):
                for g in range(2):
                    V.scalar_tensor_tensor(out=y1[:, g, :], in0=y1[:, g, :], scalar=mv[0][:, g, 0:1], in1=gamr[:, :],
                                           op0=ALU.subtract, op1=ALU.mult).then_inc(s_g1, 1)

            def gat_norm(q):
                dve.wait_ge(s_rstd[0], q + 1)
                dve.wait_ge(s_xb, q + 1)
                for g in range(2):
                    dve.wait_ge(s_g1, 2 * q + g + 1)
                    V.scalar_tensor_tensor(out=z1[:, g, :], in0=y1[:, g, :], scalar=rstd[0][:, g:g + 1],
                                           in1=xb[:, g, :], op0=ALU.mult, op1=ALU.add).then_inc(s_z1, 1)

            def second_norm(q):
                dve.wait_ge(s_rstd[1], q + 1)
                for g in range(2):
                    V.tensor_scalar(x1[:, g, :], z1[:, g, :], mv[1][:, g, 0:1], rstd[1][:, g:g + 1], ALU.subtract,
                                    ALU.mult).then_inc(s_x1, 1)

            def v_out(q):
                dve.wait_ge(s_vmm, q + 1)
                V.tensor_tensor(v[:, :, :], v_ps, bvr[:, :].unsqueeze(1).to_broadcast([128, 2, F]),
                                ALU.add).then_inc(s_v, 1)

            def max3(q, g):
                dve.wait_ge(s_group, 8 * q + 4 * g + 4)
                V.reduce_max(mx3[g][:, :], wide[g][:, :, :].rearrange("p b (c m) -> p (b c) m", m=N), AX.X).then_inc(s_mx3, 1)
                dve.wait_ge(s_mx3, 2 * q + g + 1)
                V.tensor_scalar(nb3[g][:, :], mx3[g][:, :], -SCALE, None, ALU.mult).then_inc(s_nb3, 1)

            def recip3(q, g):
                dve.wait_ge(s_e3, AH * (2 * q + g + 1))
                V.reciprocal(r3[g][:, :], sum3[g][:, :]).then_inc(s_ri3, 1)
                dve.wait_ge(s_ri3, 2 * q + g + 1)
                V.tensor_scalar(r3[g][:, :], r3[g][:, :], row_ok[:, 2:3], None, ALU.mult).then_inc(s_r3, 1)

            def final_sum(z):
                dve.wait_ge(s_y3mm, z + 1)
                dve.wait_ge(s_x1b, z + 1)
                V.tensor_tensor(y3[:, :, :], y3_ps, x1b, ALU.add).then_inc(s_y3, 1)

            def final_norm(z):
                dve.wait_ge(s_rstd[2], z + 1)
                wait(dve, s_store, 16 * z)
                for g in range(2):
                    V.tensor_scalar(fin[:, g, :], y3[:, g, :], mv[2][:, g, 0:1], rstd[2][:, g:g + 1], ALU.subtract,
                                    ALU.mult).then_inc(s_fin, 1)

            V.memset(neg_half[:, :], -0.5).then_inc(s_const, 1)
            dve.wait_ge(s_idn, 16)
            V.tensor_copy(ident_bf[:, :], ident[:, :]).then_inc(s_masks, 1)
            dve.wait_ge(s_adj, 16)
            link(V.tensor_copy(adj_f[:, :], adj_i[:, :]))
            V.tensor_scalar(gat_mask[:, :], adj_f[:, :], 0.0, MASKED, ALU.is_le, ALU.mult).then_inc(s_masks, 1)
            V.tensor_scalar(mha_mask[:, :], adj_f[:, :], 0.0, MASKED, ALU.is_equal, ALU.mult).then_inc(s_masks, 1)
            link(V.tensor_scalar(adj_f[:, :], adj_f[:, :], 0.0, None, ALU.not_equal))
            link(V.reduce_max(row_ok[:, 0:1], adj_f[:, :], AX.X))
            link(V.reciprocal(row_ok[:, 1:2], row_ok[:, 0:1]))
            link(V.tensor_tensor(row_ok[:, 2:3], row_ok[:, 0:1], row_ok[:, 1:2], ALU.mult))
            dve.wait_ge(s_win, 16 * (1 + KT))
            for k in range(KT):
                for j in range(2):
                    view = prod[:, 0:GH, :]
                    link(V.tensor_tensor(view, w_in[:, k, NF:].rearrange("p (h o) -> p h o", h=GH),
                                         a_rows[:, :, j * F:(j + 1) * F], ALU.mult))
                    link(V.reduce_sum(w_in[:, k, j * GH:(j + 1) * GH], view, AX.X))
            split(w_in[:, :, :], w_hi[:, :, :], w_lo[:, :, :], s_wready)
            split_xt(0)

            def second_weights():
                dve.wait_ge(s_wout, 32)
                for j in range(2):
                    link(V.tensor_tensor(prod[:, :, :], wout_in[:, :, 0:F],
                                         ao_rows[:, j * F:(j + 1) * F].unsqueeze(1).to_broadcast([128, HT, F]), ALU.mult))
                    link(V.reduce_sum(wout_in[:, :, F + j:F + j + 1], prod[:, :, :], AX.X))
                split(wout_in[:, :, :], wout_hi[:, :, :], wout_lo[:, :, :], s_wready)

            def step(s, front, middle, end):
                q, z = s - 1, s - 2
                more = front and (not isinstance(s, int) or s + 1 < PAIRS)
                if end:
                    recip3(z, 0)
                if front:
                    scores1(s, 0)
                    leaky_scores1(s, 0)
                if middle:
                    elu2(q)
                if end:
                    recip3(z, 1)
                if front:
                    scores1(s, 1)
                    sums1(s, 0)
                    leaky_scores1(s, 1)
                if middle:
                    tail_out(q, s_gthi, gt_ps, gt_hi, gt_lo, s_gtlo)
                if front:
                    sums1(s, 1)
                    if isinstance(s, int) and s == 0:
                        second_weights()
                if middle:
                    hidden_tail(q)
                if front:
                    elu1(s, 0, 0)
                    elu1(s, 0, 1)
                if middle:
                    if isinstance(s, int) and s == 1:
                        dve.wait_ge(s_rows, 80)
                    gat_sum(q)
                if end:
                    tail_out(z, s_athi, at_ps, at_hi, at_lo, s_atlo)
                if middle:
                    norm_stats(0, q, y1, s_y1, 1)
                    gat_gamma(q)
                if front:
                    elu1(s, 1, 0)
                if middle:
                    gat_norm(q)
                    norm_stats(1, q, z1, s_z1, 2)
                if front:
                    elu1(s, 1, 1)
                if middle:
                    second_norm(q)
                if front:
                    elu1_last_tail(s)
                if end:
                    final_sum(z)
                if middle:
                    tail_out(q, s_x1thi, x1t_ps, x1t_hi, x1t_lo, s_x1tlo)
                if end:
                    norm_stats(2, z, y3, s_y3, 1)
                if more:
                    split_xt(s + 1)
                if end:
                    final_norm(z)
                if front:
                    scores2(s)
                    less_max2(s)
                if middle:
                    v_out(q)
                if front:
                    sums2(s)
                if middle:
                    max3(q, 0)
                    max3(q, 1)

            run_steps(dve, step)

        @block.gpsimd
        def _(pool):
            P = nc.gpsimd

            def x_beta(q):
                pool.wait_ge(s_xn, 16 * (q + 1))
                wait(pool, s_z1, 2 * q)
                P.tensor_tensor(xb[:, :, :], xn[:, :, :], betr[:, :].unsqueeze(1).to_broadcast([128, 2, F]),
                                ALU.add).then_inc(s_xb, 1)

            def less_max1(p, g):
                pool.wait_ge(s_lk1, 2 * p + g + 1)
                pool.wait_ge(s_m1, 2 * p + g + 1)
                P.tensor_tensor(e1[g][:, :, :], e1[g][:, :, :], per_head(m1[g][:, :]), ALU.subtract).then_inc(s_d1, 1)

            def normalise1(p, g):
                pool.wait_ge(s_r1, 2 * p + g + 1)
                wait(pool, s_pt1mm, 2 * (p - 1) + g + 1)
                P.tensor_tensor(p1[g][:, :, :], e1[g][:, :, :], per_head(r1[g][:, :]), ALU.mult).then_inc(s_p1, 1)

            def normalise2(q):
                pool.wait_ge(s_r2, q + 1)
                P.tensor_tensor(p2[:, :, :], e2[:, :, :], per_head(r2[:, :]), ALU.mult).then_inc(s_p2, 1)

            def elu1_tail(p, g, half):
                part = slice(4 * half, 4 * half + 4)
                pool.wait_ge(s_hhi, 4 * p + 2 * g + half + 1)
                P.tensor_tensor(ht_lo[g][:, part, :], em[g][:, part, :], ht_hi[g][:, part, :].bitcast(fp32),
                                ALU.subtract).then_inc(s_hlo, 1)

            def gat_plus_b2(q):
                pool.wait_ge(s_gat, q + 1)
                P.tensor_tensor(gat_b2[:, :, :], gat[:, :, :], b2r[:, :].unsqueeze(1).to_broadcast([128, 2, F]),
                                ALU.add).then_inc(s_gatb2, 1)

            def inverse_std(i, q):
                pool.wait_ge(s_ve[i], q + 1)
                P.tensor_tensor(rstd[i][:, :], ve[i][:, :], neg_half[:, :], ALU.pow).then_inc(s_rstd[i], 1)

            def x1_plus_bo(q):
                pool.wait_ge(s_x1, 2 * q + 2)
                wait(pool, s_y3, q)
                P.tensor_tensor(x1b[:, :, :], x1[:, :, :], bor[:, :].unsqueeze(1).to_broadcast([128, 2, F]),
                                ALU.add).then_inc(s_x1b, 1)

            def normalise3(q, g):
                pool.wait_ge(s_r3, 2 * q + g + 1)
                for b in range(2):
                    part = slice(4 * b, 4 * b + 4)
                    P.tensor_tensor(p3[g][:, part, :], e3[g][:, part, :], per_head(r3[g][:, part]),
                                    ALU.mult).then_inc(s_p3, 1)

            for i, (name, (hi, lo)) in enumerate(small.items()):
                pool.wait_ge(s_smallhi, i + 1)
                P.tensor_tensor(lo[:, :, :], small_in[name], hi[:, :, :].bitcast(fp32), ALU.subtract).then_inc(s_smallw, 1)
            pool.wait_ge(s_rows, 80)
            pool.wait_ge(s_const, 1)

            def step(s, front, middle, end):
                q, z = s - 1, s - 2
                if end:
                    normalise3(z, 0)
                if front:
                    less_max1(s, 0)
                if end:
                    normalise3(z, 1)
                if front:
                    normalise1(s, 0)
                    less_max1(s, 1)
                if middle:
                    gat_plus_b2(q)
                if front:
                    normalise1(s, 1)
                if middle:
                    x_beta(q)
                if front:
                    elu1_tail(s, 0, 0)
                if middle:
                    inverse_std(0, q)
                if front:
                    elu1_tail(s, 0, 1)
                    elu1_tail(s, 1, 0)
                if middle:
                    inverse_std(1, q)
                    x1_plus_bo(q)
                if end:
                    inverse_std(2, z)
                if front:
                    normalise2(s)

            run_steps(pool, step)


def kernel(**inputs):
    import numpy as np
    import concourse.bacc as bacc
    from concourse import mybir as mb
    from concourse.bass_utils import run_bass_kernel_spmd

    a = {k: np.ascontiguousarray(v) for k, v in inputs.items()}
    x = a["x"]
    B, n, f = x.shape

    def columns(v):
        return np.ascontiguousarray(v.reshape(-1, 128).T)

    arrays = {
        "x_t": np.ascontiguousarray(x.reshape(B // 2, 2, n, f // 128, 128).transpose(0, 4, 3, 1, 2)),
        "x": x,
        "adj": a["adj"],
        "w_heads": a["L0_gnn_W_heads"],
        "a_heads": a["L0_gnn_a_heads"],
        "w_out": a["L0_gnn_W_out"],
        "a_out": a["L0_gnn_a_out"],
        "w1": a["L0_gnn_w1"],
        "b1_cols": columns(a["L0_gnn_b1"]),
        "w2": a["L0_gnn_w2"],
        "b2": a["L0_gnn_b2"],
        "ln_gamma": a["L0_gnn_ln_gamma"],
        "ln_beta": a["L0_gnn_ln_beta"],
        "wq_t": np.ascontiguousarray(a["L1_gnn_Wq"].T),
        "bq_cols": columns(a["L1_gnn_bq"]),
        "wk_t": np.ascontiguousarray(a["L1_gnn_Wk"].T),
        "bk_cols": columns(a["L1_gnn_bk"]),
        "wv_t": np.ascontiguousarray(a["L1_gnn_Wv"].T),
        "bv": a["L1_gnn_bv"],
        "wo_t": np.ascontiguousarray(a["L1_gnn_Wo"].T),
        "bo": a["L1_gnn_bo"],
        "identity": np.eye(128, dtype=np.float32),
    }
    nc = bacc.Bacc("TRN2", target_bir_lowering=False, num_devices=1)
    args = [nc.dram_tensor(k, v.shape, mb.dt.from_np(v.dtype), kind="ExternalInput").ap() for k, v in arrays.items()]
    out = nc.dram_tensor("out", (B, n, f), mb.dt.float32, kind="ExternalOutput").ap()
    gat_then_attention_kernel(nc, *args, out)
    r = run_bass_kernel_spmd(nc, [arrays], core_ids=[0])
    return r.results[0]["out"]
```

```python
import concourse.bass as bass
from concourse import mybir
from contextlib import ExitStack


def gat_then_attention_kernel(nc: bass.Bass, x_t, x, adj, w_heads, a_heads, w_out, a_out, w1, b1_cols, w2, b2,
                              ln_gamma, ln_beta, wq_t, bq_cols, wk_t, bk_cols, wv_t, bv, wo_t, bo, identity, out):
    fp32 = mybir.dt.float32
    fp32r = mybir.dt.float32r
    bf16 = mybir.dt.bfloat16
    i32 = mybir.dt.int32
    ALU = mybir.AluOpType
    ACT = mybir.ActivationFunctionType
    AX = mybir.AxisListType

    N = 128
    F = x.shape[2]
    KT = F // 128
    PAIRS = x.shape[0] // 2
    GH = w_heads.shape[0]
    HF = GH * F
    HT = HF // 128
    AH = 8
    D = F // AH
    SCALE = float(D) ** -0.5
    LEAKY = 0.01
    EPS = 1e-5
    MASKED = -1e30
    NF = 2 * GH
    WC = NF + HF
    CH = 3
    CW = WC // CH
    assert CW * CH == WC and CW <= 512
    F2 = F + 2

    ctx = ExitStack()
    with ctx:
        def sb(name, shape, dt=fp32):
            return ctx.enter_context(nc.sbuf_tensor(name, shape, dt))

        def ps(name, shape):
            return ctx.enter_context(nc.psum_tensor(name, shape, fp32))

        def sem(name):
            return ctx.enter_context(nc.semaphore(name))

        ident = sb("ident", [128, 128])
        ident_bf = sb("ident_bf", [128, 128], bf16)
        adj_i = sb("adj_i", [128, N], i32)
        adj_f = sb("adj_f", [128, N])
        gat_mask = sb("gat_mask", [128, N], bf16)
        mha_mask = sb("mha_mask", [128, N], bf16)
        row_ok = sb("row_ok", [128, 3])
        ao_rows = sb("ao_rows", [128, 2 * F])
        small_names = ("w1", "w2", "wq", "wk", "wv", "wo")
        w_hi, w_lo = sb("w_hi", [128, KT, WC], fp32r), sb("w_lo", [128, KT, WC], fp32r)
        wout_hi, wout_lo = sb("wout_hi", [128, HT, F2], fp32r), sb("wout_lo", [128, HT, F2], fp32r)
        small = {k: (sb(k + "_hi", [128, KT, F], fp32r), sb(k + "_lo", [128, KT, F], fp32r)) for k in small_names}
        b1c, bqc, bkc = sb("b1c", [128, KT]), sb("bqc", [128, KT]), sb("bkc", [128, KT])
        b2r, gamr, betr, bvr, bor = (sb(n, [128, F]) for n in ("b2r", "gamr", "betr", "bvr", "bor"))
        neg_half = sb("neg_half", [128, 2])

        xt = sb("xt", [128, KT, 2, N])
        xt_hi, xt_lo = sb("xt_hi", [128, KT, 2, N], fp32r), sb("xt_lo", [128, KT, 2, N], fp32r)
        wh = [sb(f"wh{g}", [128, WC]) for g in range(2)]
        gat_probs = sb("gat_probs", [128, 3 * 2 * GH * N])
        t1, e1, p1 = ([gat_probs[:, (2 * i + g) * GH * N:(2 * i + g + 1) * GH * N].rearrange("p (h m) -> p h m", m=N)
                       for g in range(2)] for i in range(3))
        pt1 = [sb(f"pt1_{g}", [128, GH, N]) for g in range(2)]
        mx1 = [sb(f"mx1_{g}", [128, GH]) for g in range(2)]
        m1 = [sb(f"m1_{g}", [128, GH]) for g in range(2)]
        nm1 = [sb(f"nm1_{g}", [128, GH]) for g in range(2)]
        sum1 = [sb(f"sum1_{g}", [128, GH]) for g in range(2)]
        r1 = [sb(f"r1_{g}", [128, GH]) for g in range(2)]
        elu_in = sb("elu_in", [128, max(2 * HT * N, KT * WC)])
        em = [elu_in[:, g * HT * N:(g + 1) * HT * N].rearrange("p (t n) -> p t n", n=N) for g in range(2)]
        ht_hi = [sb(f"ht_hi{g}", [128, HT, N], fp32r) for g in range(2)]
        ht_lo = [sb(f"ht_lo{g}", [128, HT, N], fp32r) for g in range(2)]
        wh2 = sb("wh2", [128, 2, F2])

        xn = sb("xn", [128, 2, F])
        xb = sb("xb", [128, 2, F])
        t2, e2, p2, pt2 = (sb(n, [128, 2, N]) for n in ("t2", "e2", "p2", "pt2"))
        mx2, m2, nm2, sum2, r2 = (sb(n, [128, 2]) for n in ("mx2", "m2", "nm2", "sum2", "r2"))
        em2, gat = sb("em2", [128, 2, F]), sb("gat", [128, 2, F])
        row_bufs = sb("row_bufs", [128, 6 * 2 * F])
        gat_b2, y1, z1, x1, x1b, v = (row_bufs[:, i * 2 * F:(i + 1) * 2 * F].rearrange("p (g f) -> p g f", g=2)
                                      for i in range(6))
        gt_hi, gt_lo = sb("gt_hi", [128, KT, 2, N], fp32r), sb("gt_lo", [128, KT, 2, N], fp32r)
        hid = sb("hid", [128, KT, 2, N])
        hid_hi, hid_lo = sb("hid_hi", [128, KT, 2, N], fp32r), sb("hid_lo", [128, KT, 2, N], fp32r)
        stats = [sb(f"stats{i}", [128, 2, 6]) for i in range(3)]
        mv = [sb(f"mv{i}", [128, 2, 2]) for i in range(3)]
        ve = [sb(f"ve{i}", [128, 2]) for i in range(3)]
        rstd = [sb(f"rstd{i}", [128, 2]) for i in range(3)]
        x1t_hi, x1t_lo = sb("x1t_hi", [128, KT, 2, N], fp32r), sb("x1t_lo", [128, KT, 2, N], fp32r)
        qt, kt = sb("qt", [128, KT, 2, N]), sb("kt", [128, KT, 2, N])
        mx3 = [sb(f"mx3_{g}", [128, AH]) for g in range(2)]
        nb3 = [sb(f"nb3_{g}", [128, AH]) for g in range(2)]
        sum3 = [sb(f"sum3_{g}", [128, AH]) for g in range(2)]
        r3 = [sb(f"r3_{g}", [128, AH]) for g in range(2)]
        mha_probs = sb("mha_probs", [128, max(6 * AH * N, 4 * AH * N + HT * F2)])
        e3, p3, pt3 = ([mha_probs[:, (2 * i + g) * AH * N:(2 * i + g + 1) * AH * N].rearrange("p (h m) -> p h m", m=N)
                        for g in range(2)] for i in range(3))
        at_hi, at_lo = sb("at_hi", [128, KT, 2, N], fp32r), sb("at_lo", [128, KT, 2, N], fp32r)
        y3, fin = sb("y3", [128, 2, F]), sb("fin", [128, 2, F])

        small_in = {k: row_bufs[:, i * KT * F:(i + 1) * KT * F].rearrange("p (t o) -> p t o", t=KT)
                    for i, k in enumerate(small_names)}
        w_in = elu_in[:, 0:KT * WC].rearrange("p (t c) -> p t c", t=KT)
        a_rows = mha_probs[:, 0:2 * GH * F].rearrange("p (h j) -> p h j", h=GH)
        prod = mha_probs[:, 2 * GH * F:2 * GH * F + HT * F].rearrange("p (t o) -> p t o", t=HT)
        wout_in = mha_probs[:, 4 * GH * F:4 * GH * F + HT * F2].rearrange("p (t c) -> p t c", t=HT)

        tri = ps("tri", [128, 3, 512])
        mid = ps("mid", [128, 512])
        wide_b = ps("wide_b", [128, 2, 512])
        wide_a = ps("wide_a", [128, 2, 512])
        wide = [wide_a, wide_b]

        def heads(bank):
            return bank.rearrange("p (h m) -> p h m", m=N)

        s1_ps = pt1_ps = heads(mid[:, :])
        s2_ps = pt2_ps = heads(mid[:, 0:2 * N])
        wh2_ps = [mid[:, 0:F2], tri[:, 1, 0:F2]]
        gat_ps = wide_a[:, 0, :].rearrange("p (g f) -> p g f", g=2)
        gt_ps = wide_a[:, 1, :].rearrange("p (t g n) -> p t g n", t=KT, g=2)
        pt3_ps = [wide_b[:, :, :], tri[:, 0:2, :]]
        tri_t = [tri[:, c, :].rearrange("p (t g n) -> p t g n", t=KT, g=2) for c in range(3)]
        tri_g = [tri[:, c, :].rearrange("p (g f) -> p g f", g=2) for c in range(3)]
        at_ps, x1t_ps, v_ps = tri_t[0], tri_t[0], tri_g[0]
        y1_ps, q_ps = tri_g[1], tri_t[1]
        hid_ps, y3_ps, k_ps = tri_t[2], tri_g[2], tri_t[2]

        s_adj, s_arows, s_wout, s_small, s_rows, s_cols = (
            sem("load_" + n) for n in ("adj", "a_heads", "w_out", "small", "rows", "cols"))
        s_win = [sem(f"load_w_in{k}") for k in range(KT)]
        s_idn, s_const, s_masks, s_dsc, s_wready, s_wtail = (
            sem(n) for n in ("ident_loaded", "constants_ready", "masks_ready", "setup_chain", "score_columns_ready",
                             "weight_tails_ready"))
        s_whead = sem("weight_heads_ready")
        s_group = sem("score_row_group_done")
        s_passed = sem("waits_passed")
        s_xt, s_xn, s_store = sem("xt_loaded"), sem("xn_loaded"), sem("out_stored")
        s_xhi, s_xsplit = sem("xt_hi_ready"), sem("xt_split")
        s_whmm, s_wh = sem("wh_mm"), sem("wh_ready")
        s_s1, s_t1, s_mx1, s_lk1, s_m1, s_nm1, s_e1 = (
            sem(n) for n in ("s1_mm", "t1_ready", "mx1_ready", "leaky1", "m1_ready", "minus_m1_ready", "e1_ready"))
        s_r1, s_p1, s_pt1mm, s_pt1 = (sem(n) for n in ("r1_ready", "p1_ready", "pt1_mm", "pt1_ready"))
        s_htmm, s_eh, s_em, s_h, s_hhi = (
            sem(n) for n in ("ht_mm", "eh_ready", "em_ready", "h_ready", "ht_hi_ready"))
        s_hlo, s_hlo1b = sem("ht_lo_ready"), sem("ht_lo_graph1_second_half_ready")
        s_wh2mm, s_wh2 = sem("wh2_mm"), sem("wh2_ready")
        s_xb = sem("xb_ready")
        s_s2, s_t2, s_mx2, s_lk2, s_m2, s_nm2, s_e2, s_r2, s_p2, s_pt2mm, s_pt2 = (
            sem(n) for n in ("s2_mm", "t2_ready", "mx2_ready", "leaky2", "m2_ready", "minus_m2_ready", "e2_ready",
                             "r2_ready", "p2_ready", "pt2_mm", "pt2_ready"))
        s_gatmm, s_eo, s_em2, s_gat, s_gatb2, s_gtmm, s_gthi, s_gtlo = (
            sem(n) for n in ("gat_mm", "eo_ready", "em2_ready", "gat_ready", "gat_b2_ready", "gt_mm", "gt_hi_ready",
                             "gt_lo_ready"))
        s_hidmm, s_hid, s_hidhi, s_hidlo, s_y1mm, s_y1 = (
            sem(n) for n in ("hid_mm", "hid_ready", "hid_hi_ready", "hid_lo_ready", "y1_mm", "y1_ready"))
        s_st = [sem(f"stats{i}_ready") for i in range(3)]
        s_mv = [sem(f"mv{i}_ready") for i in range(3)]
        s_ve = [sem(f"var_eps{i}_ready") for i in range(3)]
        s_rstd = [sem(f"rstd{i}_ready") for i in range(3)]
        s_g1, s_z1, s_x1, s_x1b = (sem(n) for n in ("y1_gamma", "z1_ready", "x1_ready", "x1b_ready"))
        s_x1tmm, s_x1thi, s_x1tlo = sem("x1t_mm"), sem("x1t_hi_ready"), sem("x1t_lo_ready")
        s_qmm, s_kmm, s_vmm, s_qt, s_kt, s_v = (
            sem(n) for n in ("q_mm", "k_mm", "v_mm", "q_ready", "k_ready", "v_ready"))
        s_mx3, s_nb3, s_e3, s_ri3, s_r3, s_p3, s_pt3mm = (
            sem(n) for n in ("mx3_ready", "nb3_ready", "e3_ready", "recip3", "r3_ready", "p3_ready",
                             "pt3_mm"))
        s_pt3 = [sem(f"pt3_ready{g}") for g in range(2)]
        s_atmm, s_athi, s_atlo, s_y3mm, s_y3, s_fin = (
            sem(n) for n in ("at_mm", "at_hi_ready", "at_lo_ready", "y3_mm", "y3_ready", "fin_ready"))

        def wait(eng, semaphore, value):
            if not isinstance(value, int) or value > 0:
                eng.wait_ge(semaphore, value)

        def wait_apart(eng, semaphore, value):
            wait(eng, semaphore, value)
            eng.sem_inc(s_passed, 1)

        def per_head(column, n=N):
            return column.unsqueeze(2).to_broadcast([128, column.shape[1], n])

        def run_steps(eng, step):
            for s in range(3):
                step(s, True, s >= 1, s >= 2)
            with eng.Fori(3, PAIRS - 1) as s:
                step(s, True, True, True)
            step(PAIRS - 1, True, True, True)
            step(PAIRS, False, True, True)
            step(PAIRS + 1, False, False, True)

        block = ctx.enter_context(nc.Block())

        @block.sync
        def _(sp):
            def load_xt(p):
                wait(sp, s_xsplit, p)
                sp.dma_start(xt[:, :, :, :], x_t[p]).then_inc(s_xt, 16)

            sp.dma_start(adj_i[:, :], adj).then_inc(s_adj, 16)
            sp.dma_start(ident[:, :], identity).then_inc(s_idn, 16)
            load_xt(0)
            sp.dma_start(a_rows[:, :, :], a_heads.unsqueeze(0).to_broadcast([128, GH, 2 * F])).then_inc(s_arows, 16)
            for k in range(KT):
                sp.dma_start(w_in[:, k, NF:].rearrange("p (h o) -> p h o", h=GH),
                             w_heads[:, k * 128:(k + 1) * 128, :].rearrange("h p o -> p h o")).then_inc(s_win[k], 16)
            sp.dma_start(ao_rows[:, :], a_out.unsqueeze(0).to_broadcast([128, 2 * F])).then_inc(s_wout, 16)
            sp.dma_start(wout_in[:, :, 0:F], w_out.rearrange("(t p) o -> p t o", p=128)).then_inc(s_wout, 16)
            for name, w in (("w1", w1), ("w2", w2), ("wq", wq_t), ("wk", wk_t), ("wv", wv_t), ("wo", wo_t)):
                sp.dma_start(small_in[name][:, :, :], w.rearrange("(t p) o -> p t o", p=128)).then_inc(s_small, 16)
            for dst, src in ((b1c, b1_cols), (bqc, bq_cols), (bkc, bk_cols)):
                sp.dma_start(dst[:, :], src).then_inc(s_cols, 16)
            for dst, src in ((b2r, b2), (gamr, ln_gamma), (betr, ln_beta), (bvr, bv), (bor, bo)):
                sp.dma_start(dst[:, :], src.unsqueeze(0).to_broadcast([128, F])).then_inc(s_rows, 16)

            def step(s, front, middle, end):
                if front:
                    if not isinstance(s, int) or s + 1 < PAIRS:
                        load_xt(s + 1)
                    wait(sp, s_xb, s)
                    sp.dma_start(xn[:, :, :], x[bass.ds(2 * s, 2)].rearrange("g n f -> n g f")).then_inc(s_xn, 16)
                if end:
                    sp.wait_ge(s_fin, 2 * s - 2)
                    sp.dma_start(out[bass.ds(2 * s - 4, 2)].rearrange("g n f -> n g f"), fin[:, :, :]).then_inc(s_store, 16)

            run_steps(sp, step)
            sp.wait_ge(s_store, 16 * PAIRS)

        @block.tensor
        def _(pe):
            def split_mm(dst, hi_l, lo_l, hi_r, lo_r, first, last):
                nc.tensor.matmul(dst, lo_l, hi_r, start=first, stop=False)
                nc.tensor.matmul(dst, hi_l, lo_r, start=False, stop=False)
                return nc.tensor.matmul(dst, hi_l, hi_r, start=False, stop=last)

            def first_features(p, g, c):
                if g == 0 and c == 0:
                    pe.wait_ge(s_xsplit, p + 1)
                    wait(pe, s_v, p - 1)
                if g == 0 and c == 1:
                    wait(pe, s_qt, 2 * (p - 1))
                if g == 0 and c == 2:
                    wait(pe, s_kt, 2 * (p - 1))
                if g == 1:
                    pe.wait_ge(s_wh, 6 * p + c + 1)
                for k in range(KT):
                    cols = slice(c * CW, (c + 1) * CW)
                    last = split_mm(tri[:, c, 0:CW], xt_hi[:, k, g, :], xt_lo[:, k, g, :], w_hi[:, k, cols],
                                    w_lo[:, k, cols], k == 0, k == KT - 1)
                last.then_inc(s_whmm, 1)

            def gat_scores1(p, g):
                pe.wait_ge(s_wh, 6 * p + 3 * g + 1)
                if g == 0:
                    wait(pe, s_pt2, p)
                else:
                    pe.wait_ge(s_t1, GH * (2 * p + 1))
                for h in range(GH):
                    last = nc.tensor.transpose(s1_ps[:, h, :], wh[g][:, GH + h:GH + h + 1].to_broadcast([128, 128]),
                                               ident[:, :])
                last.then_inc(s_s1, 1)

            def transpose_p1(p, g):
                if g == 0:
                    pe.wait_ge(s_t1, GH * (2 * p + 2))
                else:
                    pe.wait_ge(s_pt1, 2 * p + 1)
                for h in range(GH):
                    if h % 2 == 0:
                        pe.wait_ge(s_p1, 4 * p + 2 * g + h // 2 + 1)
                    last = nc.tensor.transpose(pt1_ps[:, h, :], p1[g][:, h, :], ident[:, :])
                last.then_inc(s_pt1mm, 1)

            def gat_values1(p, g):
                pe.wait_ge(s_pt1, 2 * p + g + 1)
                pe.wait_ge(s_wh, 6 * p + 3 * g + 3)
                if g == 0:
                    wait(pe, s_gtlo, p)
                else:
                    wait(pe, s_pt3[0], 2 * (p - 1))
                for t in range(HT):
                    dst = wide[g][:, t // 4, (t % 4) * N:(t % 4 + 1) * N]
                    last = nc.tensor.matmul(dst, wh[g][:, NF + t * 128:NF + (t + 1) * 128], pt1[g][:, t // KT, :],
                                            start=True, stop=True)
                    if t % 4 == 3:
                        last.then_inc(s_htmm, 1)

            def second_features(p, g, half):
                pe.wait_ge(s_hhi, 4 * p + 2 * g + half + 1)
                if half == 0 and g == 0:
                    pe.wait_ge(s_pt1, 2 * p + 2)
                if half == 0 and g == 1:
                    wait(pe, s_y1, p)
                tiles = range(4 * half, 4 * half + 4)
                for t in tiles:
                    nc.tensor.matmul(wh2_ps[g], ht_hi[g][:, t, :], wout_lo[:, t, :], start=(t == 0), stop=False)
                    nc.tensor.matmul(wh2_ps[g], ht_hi[g][:, t, :], wout_hi[:, t, :], start=False, stop=False)
                if g == 1 and half == 1:
                    pe.wait_ge(s_hlo1b, p + 1)
                else:
                    pe.wait_ge(s_hlo, 3 * p + 2 * g + half + 1)
                for t in tiles:
                    last = nc.tensor.matmul(wh2_ps[g], ht_lo[g][:, t, :], wout_hi[:, t, :], start=False,
                                            stop=(t == HT - 1))
                if half == 1:
                    last.then_inc(s_wh2mm, 1)

            def gat_scores2(p):
                pe.wait_ge(s_wh2, 2 * p + 2)
                for g in range(2):
                    last = nc.tensor.transpose(s2_ps[:, g, :], wh2[:, g, F + 1:F + 2].to_broadcast([128, 128]),
                                               ident[:, :])
                last.then_inc(s_s2, 1)

            def transpose_p2(q):
                pe.wait_ge(s_p2, q + 1)
                for g in range(2):
                    last = nc.tensor.transpose(pt2_ps[:, g, :], p2[:, g, :], ident[:, :])
                last.then_inc(s_pt2mm, 1)

            def gat_values2(q):
                pe.wait_ge(s_pt2, q + 1)
                wait(pe, s_e3, AH * (2 * q - 1))
                for g in range(2):
                    last = nc.tensor.matmul(gat_ps[:, g, :], pt2[:, g, :], wh2[:, g, 0:F], start=True, stop=True)
                last.then_inc(s_gatmm, 1)

            def transpose_gat(q):
                pe.wait_ge(s_gat, q + 1)
                for t in range(KT):
                    for g in range(2):
                        last = nc.tensor.transpose(gt_ps[:, t, g, :], gat[:, g, t * 128:(t + 1) * 128], ident[:, :])
                last.then_inc(s_gtmm, 1)

            def transposed_product(dst, weight, hi, lo, lo_ready, count):
                w_h, w_l = small[weight]
                for m in range(KT):
                    cols = slice(m * 128, (m + 1) * 128)
                    for k in range(KT):
                        nc.tensor.matmul(dst[:, m, :, :], w_l[:, k, cols], hi[:, k, :, :], start=(k == 0), stop=False)
                        nc.tensor.matmul(dst[:, m, :, :], w_h[:, k, cols], hi[:, k, :, :], start=False, stop=False)
                    if m == 0:
                        pe.wait_ge(lo_ready, count)
                    for k in range(KT):
                        last = nc.tensor.matmul(dst[:, m, :, :], w_h[:, k, cols], lo[:, k, :, :], start=False,
                                                stop=(k == KT - 1))
                return last

            def natural_rows(g, dst, weight, hi, lo, lo_ready, count):
                w_h, w_l = small[weight]
                for k in range(KT):
                    nc.tensor.matmul(dst[:, g, :], hi[:, k, g, :], w_l[:, k, :], start=(k == 0), stop=False)
                    nc.tensor.matmul(dst[:, g, :], hi[:, k, g, :], w_h[:, k, :], start=False, stop=False)
                if g == 0:
                    pe.wait_ge(lo_ready, count)
                for k in range(KT):
                    last = nc.tensor.matmul(dst[:, g, :], lo[:, k, g, :], w_h[:, k, :], start=False,
                                            stop=(k == KT - 1))
                return last

            def natural_product(*operands):
                natural_rows(0, *operands)
                return natural_rows(1, *operands)

            def ffn_up(q, front):
                pe.wait_ge(s_gthi, q + 1)
                if front:
                    pe.wait_ge(s_wh, 6 * q + 12)
                transposed_product(hid_ps, "w1", gt_hi, gt_lo, s_gtlo, q + 1).then_inc(s_hidmm, 1)

            def ffn_down(q):
                pe.wait_ge(s_hidhi, q + 1)
                wait(pe, s_pt3[1], 2 * q)
                natural_product(y1_ps, "w2", hid_hi, hid_lo, s_hidlo, q + 1).then_inc(s_y1mm, 1)

            def transpose_x1(q):
                wait(pe, s_atlo, q)
                for g in range(2):
                    pe.wait_ge(s_x1, 2 * q + g + 1)
                    for t in range(KT):
                        last = nc.tensor.transpose(x1t_ps[:, t, g, :], x1[:, g, t * 128:(t + 1) * 128], ident[:, :])
                last.then_inc(s_x1tmm, 1)

            def keys(q):
                pe.wait_ge(s_x1thi, q + 1)
                wait(pe, s_y3, q)
                transposed_product(k_ps, "wk", x1t_hi, x1t_lo, s_x1tlo, q + 1).then_inc(s_kmm, 1)

            def queries(q, front):
                if front:
                    pe.wait_ge(s_wh2, 2 * q + 4)
                transposed_product(q_ps, "wq", x1t_hi, x1t_lo, s_x1tlo, q + 1).then_inc(s_qmm, 1)

            def values3(q, g):
                natural_rows(g, v_ps, "wv", x1t_hi, x1t_lo, s_x1tlo, q + 1).then_inc(s_vmm, 1)

            def mha_scores(q, g, front):
                pe.wait_ge(s_qt, 2 * q + 2)
                pe.wait_ge(s_kt, 2 * q + 2)
                if front:
                    pe.wait_ge(s_h, 4 * (q + 1) + 2 * g + 2)
                elif g == 1:
                    pe.wait_ge(s_pt3[0], 2 * q)
                else:
                    pe.wait_ge(s_gtlo, q + 1)
                for b in range(2):
                    nc.tensor.matmul(heads(wide[g][:, b, :]), ident_bf[:, :],
                                     mha_mask[:, :].unsqueeze(1).to_broadcast([128, 4, N]), start=True, stop=False,
                                     skip_group_check=True)
                for r in range(4):
                    rows = slice(32 * r, 32 * r + 32)
                    if r >= 2:
                        pe.wait_ge(s_group, 8 * q + 4 * g + r - 1)
                    for t in range(KT):
                        b, c = head_place(r, t)
                        last = nc.tensor.matmul(wide[g][:, b, c * N:(c + 1) * N], qt[rows, t, g, :], kt[rows, t, g, :],
                                                start=False, stop=(r >= 2 and t == KT - 1), skip_group_check=True)
                    last.then_inc(s_group, 1)

            def transpose_p3(z, g, front):
                if g == 0:
                    pe.wait_ge(s_e3, AH * (2 * z + 2))
                for b in range(2):
                    if g == 1 and front:
                        pe.wait_ge(s_wh, 6 * (z + 2) + 4 + b)
                    if g == 1 and not front and b == 0:
                        pe.wait_ge(s_v, z + 1)
                    pe.wait_ge(s_p3, 4 * z + 2 * g + b + 1)
                    for c in range(4):
                        last = nc.tensor.transpose(pt3_ps[g][:, b, c * N:(c + 1) * N], p3[g][:, 4 * b + c, :],
                                                   ident[:, :])
                    last.then_inc(s_pt3mm, 1)

            def mha_values(z):
                pe.wait_ge(s_v, z + 1)
                for g in range(2):
                    pe.wait_ge(s_pt3[g], 2 * z + 2)
                for g in range(2):
                    for t in range(KT):
                        for r in range(4):
                            b, c = head_place(r, t)
                            head = 4 * t + r
                            last = nc.tensor.matmul(at_ps[32 * r:32 * r + 32, t, g, :], v[:, g, head * D:(head + 1) * D],
                                                    pt3[g][:, 4 * b + c, :], start=True, stop=True)
                last.then_inc(s_atmm, 1)

            def out_projection(q, middle):
                if middle:
                    pe.wait_ge(s_hid, 2 * q + 4)
                pe.wait_ge(s_athi, q + 1)
                natural_product(y3_ps, "wo", at_hi, at_lo, s_atlo, q + 1).then_inc(s_y3mm, 1)

            def head_place(r, t):
                return r % 2, 2 * (r // 2) + t

            pe.wait_ge(s_idn, 16)
            pe.wait_ge(s_masks, 3)
            pe.wait_ge(s_wready, 1)
            pe.wait_ge(s_wtail, KT)

            def step(s, front, middle, end):
                q, z = s - 1, s - 2
                if front:
                    first_features(s, 0, 0)
                if middle:
                    transpose_p2(q)
                if front:
                    first_features(s, 0, 1)
                    first_features(s, 0, 2)
                    gat_scores1(s, 0)
                if middle:
                    gat_values2(q)
                if front:
                    first_features(s, 1, 0)
                    first_features(s, 1, 1)
                    first_features(s, 1, 2)
                    gat_scores1(s, 1)
                if end:
                    transpose_p3(z, 0, front)
                if middle:
                    transpose_gat(q)
                if end:
                    transpose_p3(z, 1, front)
                if front:
                    transpose_p1(s, 0)
                if middle:
                    if isinstance(s, int) and s == 1:
                        pe.wait_ge(s_wtail, KT + 1 + len(small))
                    ffn_up(q, front)
                if front:
                    gat_values1(s, 0)
                if end:
                    mha_values(z)
                if front:
                    transpose_p1(s, 1)
                if middle:
                    ffn_down(q)
                if front:
                    gat_values1(s, 1)
                    if isinstance(s, int) and s == 0:
                        pe.wait_ge(s_wready, 2)
                        pe.wait_ge(s_wtail, KT + 1)
                    second_features(s, 0, 0)
                if end:
                    out_projection(z, middle)
                if front:
                    second_features(s, 0, 1)
                    second_features(s, 1, 0)
                if middle:
                    transpose_x1(q)
                if front:
                    second_features(s, 1, 1)
                if middle:
                    keys(q)
                    queries(q, front)
                if front:
                    gat_scores2(s)
                if middle:
                    values3(q, 0)
                    mha_scores(q, 0, front)
                    values3(q, 1)
                    mha_scores(q, 1, front)

            run_steps(pe, step)

        @block.scalar
        def _(act):
            def wh_out(p, g, c):
                act.wait_ge(s_whmm, 6 * p + 3 * g + c + 1)
                wait(act, s_htmm, 4 * (p - 1) + 2 * g + 2)
                nc.scalar.activation(wh[g][:, c * CW:(c + 1) * CW], tri[:, c, 0:CW], ACT.Copy).then_inc(s_wh, 1)

            def exp1(p, g):
                act.wait_ge(s_lk1, 2 * p + g + 1)
                act.wait_ge(s_nm1, 2 * p + g + 1)
                for h in range(GH):
                    nc.scalar.activation(e1[g][:, h, :], e1[g][:, h, :], ACT.Exp, bias=nm1[g][:, h:h + 1],
                                         accum_out=sum1[g][:, h:h + 1]).then_inc(s_e1, 1)

            def pt1_out(p, g):
                act.wait_ge(s_pt1mm, 2 * p + g + 1)
                nc.scalar.activation(pt1[g][:, :, :], pt1_ps, ACT.Copy).then_inc(s_pt1, 1)

            def exp_values1(p, g):
                wait(act, s_hlo, 3 * (p - 1) + 2 + g)
                if g == 1:
                    wait(act, s_hlo1b, p)

                def relu(b):
                    act.wait_ge(s_htmm, 4 * p + 2 * g + b + 1)
                    nc.scalar.activation(em[g][:, 4 * b:4 * b + 4, :], heads(wide[g][:, b, :]), ACT.Relu,
                                         scale=-1.0).then_inc(s_em, 1)

                def exp(b):
                    act.wait_ge(s_em, 4 * p + 2 * g + b + 1)
                    nc.scalar.activation(em[g][:, 4 * b:4 * b + 4, :], em[g][:, 4 * b:4 * b + 4, :], ACT.Exp,
                                         scale=-1.0).then_inc(s_eh, 1)

                relu(0)
                if g == 0:
                    relu(1)
                    exp(0)
                else:
                    exp(0)
                    relu(1)
                exp(1)

            def values1_head(p, g):
                wait(act, s_wh2mm, 2 * (p - 1) + g + 1)
                for b in range(2):
                    act.wait_ge(s_h, 4 * p + 2 * g + b + 1)
                    nc.scalar.activation(ht_hi[g][:, 4 * b:4 * b + 4, :], em[g][:, 4 * b:4 * b + 4, :],
                                         ACT.Copy).then_inc(s_hhi, 1)

            def wh2_out(p, g):
                act.wait_ge(s_wh2mm, 2 * p + g + 1)
                nc.scalar.activation(wh2[:, g, :], wh2_ps[g], ACT.Copy).then_inc(s_wh2, 1)

            def exp2(q):
                act.wait_ge(s_lk2, q + 1)
                act.wait_ge(s_nm2, q + 1)
                for g in range(2):
                    nc.scalar.activation(e2[:, g, :], e2[:, g, :], ACT.Exp, bias=nm2[:, g:g + 1],
                                         accum_out=sum2[:, g:g + 1]).then_inc(s_e2, 1)

            def pt2_out(q):
                act.wait_ge(s_pt2mm, q + 1)
                nc.scalar.activation(pt2[:, :, :], pt2_ps, ACT.Copy).then_inc(s_pt2, 1)

            def exp_gat(q):
                act.wait_ge(s_gatmm, q + 1)
                nc.scalar.activation(em2[:, :, :], gat_ps, ACT.Exp).then_inc(s_eo, 1)

            def gt_hi_out(q):
                act.wait_ge(s_gtmm, q + 1)
                nc.scalar.activation(gt_hi[:, :, :, :], gt_ps, ACT.Copy).then_inc(s_gthi, 1)

            def hidden_out(q):
                act.wait_ge(s_hidmm, q + 1)
                for t in range(KT):
                    nc.scalar.activation(hid[:, t, :, :], hid_ps[:, t, :, :], ACT.Relu,
                                         bias=b1c[:, t:t + 1]).then_inc(s_hid, 1)

            def x1t_hi_out(q):
                act.wait_ge(s_x1tmm, q + 1)
                nc.scalar.activation(x1t_hi[:, :, :, :], x1t_ps, ACT.Copy).then_inc(s_x1thi, 1)

            def qk_out(q):
                for mm, src, bias, dst, done in ((s_kmm, k_ps, bkc, kt, s_kt), (s_qmm, q_ps, bqc, qt, s_qt)):
                    act.wait_ge(mm, q + 1)
                    for t in range(KT):
                        nc.scalar.activation(dst[:, t, :, :], src[:, t, :, :], ACT.Identity,
                                             bias=bias[:, t:t + 1]).then_inc(done, 1)

            def exp3(q, g, half):
                act.wait_ge(s_nb3, 2 * q + g + 1)
                for i in range(4 * half, 4 * half + 4):
                    nc.scalar.activation(e3[g][:, i, :], wide[g][:, half, (i % 4) * N:(i % 4 + 1) * N], ACT.Exp,
                                         scale=SCALE, bias=nb3[g][:, i:i + 1],
                                         accum_out=sum3[g][:, i:i + 1]).then_inc(s_e3, 1)

            def pt3_out(z):
                for b in range(2):
                    act.wait_ge(s_pt3mm, 4 * z + b + 1)
                    nc.scalar.activation(pt3[0][:, 4 * b:4 * b + 4, :], heads(pt3_ps[0][:, b, :]),
                                         ACT.Copy).then_inc(s_pt3[0], 1)

            def at_hi_out(q):
                act.wait_ge(s_atmm, q + 1)
                nc.scalar.activation(at_hi[:, :, :, :], at_ps, ACT.Copy).then_inc(s_athi, 1)

            for k in range(KT):
                act.wait_ge(s_win[k], 16)
                nc.scalar.activation(w_hi[:, k, NF:], w_in[:, k, NF:], ACT.Copy).then_inc(s_whead, 1)
            act.wait_ge(s_wout, 32)
            nc.scalar.activation(wout_hi[:, :, 0:F], wout_in[:, :, 0:F], ACT.Copy).then_inc(s_whead, 1)

            def small_heads(names):
                act.wait_ge(s_small, 16 * len(small))
                for name in names:
                    nc.scalar.activation(small[name][0][:, :, :], small_in[name], ACT.Copy).then_inc(s_whead, 1)

            act.wait_ge(s_cols, 48)

            def step(s, front, middle, end):
                q, z = s - 1, s - 2
                if front:
                    wh_out(s, 0, 0)
                if middle:
                    pt2_out(q)
                if end:
                    exp3(z, 1, 0)
                if front:
                    wh_out(s, 0, 1)
                    wh_out(s, 0, 2)
                if end:
                    exp3(z, 1, 1)
                if middle:
                    exp_gat(q)
                if front:
                    wh_out(s, 1, 0)
                    exp1(s, 0)
                    wh_out(s, 1, 1)
                if end:
                    pt3_out(z)
                if front:
                    wh_out(s, 1, 2)
                    if isinstance(s, int) and s == 0:
                        small_heads(small_names[:2])
                if middle:
                    gt_hi_out(q)
                if front:
                    pt1_out(s, 0)
                    exp1(s, 1)
                if middle:
                    hidden_out(q)
                if front:
                    exp_values1(s, 0)
                if end:
                    at_hi_out(z)
                if front:
                    pt1_out(s, 1)
                    values1_head(s, 0)
                    exp_values1(s, 1)
                    values1_head(s, 1)
                    if isinstance(s, int) and s == 0:
                        small_heads(small_names[2:])
                if middle:
                    x1t_hi_out(q)
                if front:
                    wh2_out(s, 0)
                    wh2_out(s, 1)
                if middle:
                    qk_out(q)
                if front:
                    exp2(s)
                if middle:
                    exp3(q, 0, 1)
                    exp3(q, 0, 0)

            run_steps(act, step)

        @block.vector
        def _(dve):
            V = nc.vector
            chain = [0]

            def link(ins):
                chain[0] += 1
                ins.then_inc(s_dsc, 1)
                dve.wait_ge(s_dsc, chain[0])

            def split(src, hi, lo, done):
                link(V.tensor_copy(hi, src))
                V.tensor_tensor(lo, src, hi.bitcast(fp32), ALU.subtract).then_inc(done, 1)

            def split_xt(p):
                dve.wait_ge(s_xt, 16 * (p + 1))
                wait(dve, s_whmm, 6 * p)
                V.tensor_copy(xt_hi[:, :, :, :], xt[:, :, :, :]).then_inc(s_xhi, 1)
                dve.wait_ge(s_xhi, p + 1)
                V.tensor_tensor(xt_lo[:, :, :, :], xt[:, :, :, :], xt_hi[:, :, :, :].bitcast(fp32),
                                ALU.subtract).then_inc(s_xsplit, 1)

            def leaky(dst, src, done):
                V.scalar_tensor_tensor(out=dst, in0=src, scalar=LEAKY, in1=src, op0=ALU.mult,
                                       op1=ALU.max).then_inc(done, 1)

            def scores1(p, g):
                dve.wait_ge(s_s1, 2 * p + g + 1)
                for h in range(GH):
                    V.scalar_tensor_tensor(out=t1[g][:, h, :], in0=s1_ps[:, h, :], scalar=wh[g][:, h:h + 1],
                                           in1=gat_mask[:, :], op0=ALU.add, op1=ALU.add).then_inc(s_t1, 1)

            def leaky_scores1(p, g):
                dve.wait_ge(s_t1, GH * (2 * p + g + 1))
                V.reduce_max(mx1[g][:, :], t1[g][:, :, :], AX.X).then_inc(s_mx1, 1)
                wait(dve, s_p1, 4 * (p - 1) + 2 * g + 2)
                leaky(e1[g][:, :, :], t1[g][:, :, :], s_lk1)
                dve.wait_ge(s_mx1, 2 * p + g + 1)
                leaky(m1[g][:, :], mx1[g][:, :], s_m1)
                dve.wait_ge(s_m1, 2 * p + g + 1)
                V.tensor_scalar(nm1[g][:, :], m1[g][:, :], -1.0, None, ALU.mult).then_inc(s_nm1, 1)

            def sums1(p, g):
                dve.wait_ge(s_e1, GH * (2 * p + g + 1))
                wait(dve, s_p1, 4 * (p - 1) + 2 * g + 2)
                V.reciprocal(r1[g][:, :], sum1[g][:, :]).then_inc(s_r1, 1)

            def elu1(p, g, b):
                part = em[g][:, 4 * b:4 * b + 4, :]
                dve.wait_ge(s_eh, 4 * p + 2 * g + b + 1)
                V.scalar_tensor_tensor(out=part, in0=part, scalar=-1.0, in1=heads(wide[g][:, b, :]), op0=ALU.add,
                                       op1=ALU.max).then_inc(s_h, 1)

            def elu1_last_tail(p):
                dve.wait_ge(s_hhi, 4 * p + 4)
                V.tensor_tensor(ht_lo[1][:, 4:8, :], em[1][:, 4:8, :], ht_hi[1][:, 4:8, :].bitcast(fp32),
                                ALU.subtract).then_inc(s_hlo1b, 1)

            def scores2(q):
                dve.wait_ge(s_s2, q + 1)
                for g in range(2):
                    V.scalar_tensor_tensor(out=t2[:, g, :], in0=s2_ps[:, g, :], scalar=wh2[:, g, F:F + 1],
                                           in1=gat_mask[:, :], op0=ALU.add, op1=ALU.add).then_inc(s_t2, 1)
                dve.wait_ge(s_t2, 2 * q + 2)
                V.reduce_max(mx2[:, :], t2[:, :, :], AX.X).then_inc(s_mx2, 1)
                leaky(e2[:, :, :], t2[:, :, :], s_lk2)
                dve.wait_ge(s_mx2, q + 1)
                leaky(m2[:, :], mx2[:, :], s_m2)
                dve.wait_ge(s_m2, q + 1)
                V.tensor_scalar(nm2[:, :], m2[:, :], -1.0, None, ALU.mult).then_inc(s_nm2, 1)

            def sums2(q):
                dve.wait_ge(s_e2, 2 * q + 2)
                V.reciprocal(r2[:, :], sum2[:, :]).then_inc(s_r2, 1)

            def elu2(q):
                dve.wait_ge(s_eo, q + 1)
                V.tensor_scalar(em2[:, :, :], em2[:, :, :], 1.0, -1.0, ALU.min, ALU.add).then_inc(s_em2, 1)
                dve.wait_ge(s_em2, q + 1)
                V.tensor_tensor(gat[:, :, :], em2[:, :, :], gat_ps, ALU.max).then_inc(s_gat, 1)

            def pt3_out(z, b):
                dve.wait_ge(s_pt3mm, 4 * z + 2 + b + 1)
                V.tensor_copy(pt3[1][:, 4 * b:4 * b + 4, :], heads(pt3_ps[1][:, b, :])).then_inc(s_pt3[1], 1)

            def tail_out(q, head_ready, src, hi, lo, done):
                dve.wait_ge(head_ready, q + 1)
                V.tensor_tensor(lo[:, :, :, :], src, hi[:, :, :, :].bitcast(fp32), ALU.subtract).then_inc(done, 1)

            def hidden_split(q):
                dve.wait_ge(s_hid, 2 * q + 2)
                V.tensor_copy(hid_hi[:, :, :, :], hid[:, :, :, :]).then_inc(s_hidhi, 1)
                dve.wait_ge(s_hidhi, q + 1)
                V.tensor_tensor(hid_lo[:, :, :, :], hid[:, :, :, :], hid_hi[:, :, :, :].bitcast(fp32),
                                ALU.subtract).then_inc(s_hidlo, 1)

            def row_stats(i, q, src, ready, count):
                for g in range(2):
                    dve.wait_ge(ready, count * q + (g + 1 if count == 2 else 1))
                    V.bn_stats(stats[i][:, g, :], src[:, g, :]).then_inc(s_st[i], 1)

            def mean_variance(i, q):
                wait_apart(dve, s_st[i], 2 * q + 2)
                for g in range(2):
                    V.bn_aggr(mv[i][:, g, :], stats[i][:, g, :]).then_inc(s_mv[i], 1)
                dve.wait_ge(s_mv[i], 2 * q + 2)
                V.tensor_scalar(ve[i][:, :], mv[i][:, :, 1], EPS, None, ALU.add).then_inc(s_ve[i], 1)

            def gat_sum(q):
                dve.wait_ge(s_y1mm, q + 1)
                dve.wait_ge(s_gatb2, q + 1)
                V.tensor_tensor(y1, y1_ps, gat_b2, ALU.add).then_inc(s_y1, 1)

            def gat_gamma(q):
                for g in range(2):
                    V.scalar_tensor_tensor(out=y1[:, g, :], in0=y1[:, g, :], scalar=mv[0][:, g, 0:1], in1=gamr[:, :],
                                           op0=ALU.subtract, op1=ALU.mult).then_inc(s_g1, 1)

            def gat_norm(q):
                dve.wait_ge(s_rstd[0], q + 1)
                dve.wait_ge(s_xb, q + 1)
                for g in range(2):
                    dve.wait_ge(s_g1, 2 * q + g + 1)
                    V.scalar_tensor_tensor(out=z1[:, g, :], in0=y1[:, g, :], scalar=rstd[0][:, g:g + 1],
                                           in1=xb[:, g, :], op0=ALU.mult, op1=ALU.add).then_inc(s_z1, 1)

            def second_norm(q):
                dve.wait_ge(s_rstd[1], q + 1)
                for g in range(2):
                    V.tensor_scalar(x1[:, g, :], z1[:, g, :], mv[1][:, g, 0:1], rstd[1][:, g:g + 1], ALU.subtract,
                                    ALU.mult).then_inc(s_x1, 1)

            def v_out(q):
                dve.wait_ge(s_vmm, 2 * q + 2)
                V.tensor_tensor(v[:, :, :], v_ps, bvr[:, :].unsqueeze(1).to_broadcast([128, 2, F]),
                                ALU.add).then_inc(s_v, 1)

            def max3(q, g):
                dve.wait_ge(s_group, 8 * q + 4 * g + 4)
                V.reduce_max(mx3[g][:, :], wide[g][:, :, :].rearrange("p b (c m) -> p (b c) m", m=N), AX.X).then_inc(s_mx3, 1)
                dve.wait_ge(s_mx3, 2 * q + g + 1)
                V.tensor_scalar(nb3[g][:, :], mx3[g][:, :], -SCALE, None, ALU.mult).then_inc(s_nb3, 1)

            def recip3(q, g):
                dve.wait_ge(s_e3, AH * (2 * q + g + 1))
                V.reciprocal(r3[g][:, :], sum3[g][:, :]).then_inc(s_ri3, 1)
                dve.wait_ge(s_ri3, 2 * q + g + 1)
                V.tensor_scalar(r3[g][:, :], r3[g][:, :], row_ok[:, 2:3], None, ALU.mult).then_inc(s_r3, 1)

            def final_sum(z):
                dve.wait_ge(s_y3mm, z + 1)
                dve.wait_ge(s_x1b, z + 1)
                V.tensor_tensor(y3[:, :, :], y3_ps, x1b, ALU.add).then_inc(s_y3, 1)

            def final_norm(z):
                dve.wait_ge(s_rstd[2], z + 1)
                wait(dve, s_store, 16 * z)
                for g in range(2):
                    V.tensor_scalar(fin[:, g, :], y3[:, g, :], mv[2][:, g, 0:1], rstd[2][:, g:g + 1], ALU.subtract,
                                    ALU.mult).then_inc(s_fin, 1)

            V.memset(neg_half[:, :], -0.5).then_inc(s_const, 1)
            dve.wait_ge(s_idn, 16)
            V.tensor_copy(ident_bf[:, :], ident[:, :]).then_inc(s_masks, 1)
            dve.wait_ge(s_adj, 16)
            link(V.tensor_copy(adj_f[:, :], adj_i[:, :]))
            V.tensor_scalar(gat_mask[:, :], adj_f[:, :], 0.0, MASKED, ALU.is_le, ALU.mult).then_inc(s_masks, 1)
            V.tensor_scalar(mha_mask[:, :], adj_f[:, :], 0.0, MASKED, ALU.is_equal, ALU.mult).then_inc(s_masks, 1)
            link(V.tensor_scalar(adj_f[:, :], adj_f[:, :], 0.0, None, ALU.not_equal))
            link(V.reduce_max(row_ok[:, 0:1], adj_f[:, :], AX.X))
            link(V.reciprocal(row_ok[:, 1:2], row_ok[:, 0:1]))
            link(V.tensor_tensor(row_ok[:, 2:3], row_ok[:, 0:1], row_ok[:, 1:2], ALU.mult))
            split_xt(0)

            def dots(products):
                for i, (column, rows, a) in enumerate(products):
                    last = V.scalar_tensor_tensor(out=prod[:, i % HT, :], in0=rows, scalar=1.0, in1=a, op0=ALU.mult,
                                                  op1=ALU.mult, accum_out=column)
                    if i % HT == HT - 1:
                        link(last)

            dve.wait_ge(s_arows, 16)
            for k in range(KT):
                dve.wait_ge(s_win[k], 16)
                dots([(w_in[:, k, j * GH + h:j * GH + h + 1], w_in[:, k, NF + h * F:NF + (h + 1) * F],
                       a_rows[:, h, j * F:(j + 1) * F]) for j in range(2) for h in range(GH)])
            split(w_in[:, :, 0:NF], w_hi[:, :, 0:NF], w_lo[:, :, 0:NF], s_wready)
            dve.wait_ge(s_wout, 32)
            dots([(wout_in[:, t, F + j:F + j + 1], wout_in[:, t, 0:F], ao_rows[:, j * F:(j + 1) * F])
                  for t in range(HT) for j in range(2)])
            split(wout_in[:, :, F:], wout_hi[:, :, F:], wout_lo[:, :, F:], s_wready)

            def step(s, front, middle, end):
                q, z = s - 1, s - 2
                more = front and (not isinstance(s, int) or s + 1 < PAIRS)
                if end:
                    recip3(z, 0)
                if front:
                    scores1(s, 0)
                    leaky_scores1(s, 0)
                if end:
                    recip3(z, 1)
                if middle:
                    elu2(q)
                if front:
                    scores1(s, 1)
                    sums1(s, 0)
                    leaky_scores1(s, 1)
                if middle:
                    tail_out(q, s_gthi, gt_ps, gt_hi, gt_lo, s_gtlo)
                if end:
                    pt3_out(z, 0)
                if front:
                    sums1(s, 1)
                if end:
                    pt3_out(z, 1)
                if middle:
                    hidden_split(q)
                if front:
                    elu1(s, 0, 0)
                    elu1(s, 0, 1)
                if end:
                    tail_out(z, s_athi, at_ps, at_hi, at_lo, s_atlo)
                if middle:
                    if isinstance(s, int) and s == 1:
                        dve.wait_ge(s_rows, 80)
                    gat_sum(q)
                    row_stats(0, q, y1, s_y1, 1)
                    mean_variance(0, q)
                    gat_gamma(q)
                if front:
                    elu1(s, 1, 0)
                if middle:
                    gat_norm(q)
                    row_stats(1, q, z1, s_z1, 2)
                    mean_variance(1, q)
                if front:
                    elu1(s, 1, 1)
                if middle:
                    second_norm(q)
                if front:
                    elu1_last_tail(s)
                if end:
                    final_sum(z)
                if middle:
                    tail_out(q, s_x1thi, x1t_ps, x1t_hi, x1t_lo, s_x1tlo)
                if more:
                    split_xt(s + 1)
                if end:
                    row_stats(2, z, y3, s_y3, 1)
                    mean_variance(2, z)
                if front:
                    scores2(s)
                    sums2(s)
                if middle:
                    max3(q, 0)
                    v_out(q)
                if end:
                    final_norm(z)
                if middle:
                    max3(q, 1)

            run_steps(dve, step)

        @block.gpsimd
        def _(pool):
            P = nc.gpsimd

            def x_beta(q):
                pool.wait_ge(s_xn, 16 * (q + 1))
                wait(pool, s_z1, 2 * q)
                P.tensor_tensor(xb[:, :, :], xn[:, :, :], betr[:, :].unsqueeze(1).to_broadcast([128, 2, F]),
                                ALU.add).then_inc(s_xb, 1)

            def normalise1(p, g):
                pool.wait_ge(s_r1, 2 * p + g + 1)
                wait(pool, s_pt1mm, 2 * (p - 1) + g + 1)
                for half in range(2):
                    part = slice(2 * half, 2 * half + 2)
                    P.tensor_tensor(p1[g][:, part, :], e1[g][:, part, :], per_head(r1[g][:, part]),
                                    ALU.mult).then_inc(s_p1, 1)

            def normalise2(q):
                pool.wait_ge(s_r2, q + 1)
                P.tensor_tensor(p2[:, :, :], e2[:, :, :], per_head(r2[:, :]), ALU.mult).then_inc(s_p2, 1)

            def elu1_tail(p, g, half):
                part = slice(4 * half, 4 * half + 4)
                pool.wait_ge(s_hhi, 4 * p + 2 * g + half + 1)
                P.tensor_tensor(ht_lo[g][:, part, :], em[g][:, part, :], ht_hi[g][:, part, :].bitcast(fp32),
                                ALU.subtract).then_inc(s_hlo, 1)

            def gat_plus_b2(q):
                pool.wait_ge(s_gat, q + 1)
                P.tensor_tensor(gat_b2[:, :, :], gat[:, :, :], b2r[:, :].unsqueeze(1).to_broadcast([128, 2, F]),
                                ALU.add).then_inc(s_gatb2, 1)

            def inverse_std(i, q):
                pool.wait_ge(s_ve[i], q + 1)
                P.tensor_tensor(rstd[i][:, :], ve[i][:, :], neg_half[:, :], ALU.pow).then_inc(s_rstd[i], 1)

            def x1_plus_bo(q):
                pool.wait_ge(s_x1, 2 * q + 2)
                wait(pool, s_y3, q)
                P.tensor_tensor(x1b[:, :, :], x1[:, :, :], bor[:, :].unsqueeze(1).to_broadcast([128, 2, F]),
                                ALU.add).then_inc(s_x1b, 1)

            def normalise3(q, g, b):
                pool.wait_ge(s_r3, 2 * q + g + 1)
                part = slice(4 * b, 4 * b + 4)
                P.tensor_tensor(p3[g][:, part, :], e3[g][:, part, :], per_head(r3[g][:, part]),
                                ALU.mult).then_inc(s_p3, 1)

            tails = [(w_in[:, k, NF:], w_hi[:, k, NF:], w_lo[:, k, NF:]) for k in range(KT)]
            tails += [(wout_in[:, :, 0:F], wout_hi[:, :, 0:F], wout_lo[:, :, 0:F])]
            tails += [(small_in[name], hi[:, :, :], lo[:, :, :]) for name, (hi, lo) in small.items()]

            def weight_tails(first, end):
                for i in range(first, end):
                    src, hi, lo = tails[i]
                    pool.wait_ge(s_whead, i + 1)
                    P.tensor_tensor(lo, src, hi.bitcast(fp32), ALU.subtract).then_inc(s_wtail, 1)

            weight_tails(0, KT + 1)
            pool.wait_ge(s_rows, 80)
            pool.wait_ge(s_const, 1)

            def step(s, front, middle, end):
                q, z = s - 1, s - 2
                if end:
                    normalise3(z, 0, 0)
                    normalise3(z, 0, 1)
                    normalise3(z, 1, 0)
                    normalise3(z, 1, 1)
                if front:
                    normalise1(s, 0)
                if middle:
                    gat_plus_b2(q)
                if front:
                    normalise1(s, 1)
                    if isinstance(s, int) and s == 0:
                        weight_tails(KT + 1, KT + 3)
                if middle:
                    x_beta(q)
                if front:
                    elu1_tail(s, 0, 0)
                if middle:
                    inverse_std(0, q)
                if front:
                    elu1_tail(s, 0, 1)
                    elu1_tail(s, 1, 0)
                    if isinstance(s, int) and s == 0:
                        weight_tails(KT + 3, len(tails))
                if middle:
                    inverse_std(1, q)
                    x1_plus_bo(q)
                if end:
                    inverse_std(2, z)
                if front:
                    normalise2(s)

            run_steps(pool, step)


def kernel(**inputs):
    import numpy as np
    import concourse.bacc as bacc
    from concourse import mybir as mb
    from concourse.bass_utils import run_bass_kernel_spmd

    a = {k: np.ascontiguousarray(v) for k, v in inputs.items()}
    x = a["x"]
    B, n, f = x.shape

    def columns(v):
        return np.ascontiguousarray(v.reshape(-1, 128).T)

    arrays = {
        "x_t": np.ascontiguousarray(x.reshape(B // 2, 2, n, f // 128, 128).transpose(0, 4, 3, 1, 2)),
        "x": x,
        "adj": a["adj"],
        "w_heads": a["L0_gnn_W_heads"],
        "a_heads": a["L0_gnn_a_heads"],
        "w_out": a["L0_gnn_W_out"],
        "a_out": a["L0_gnn_a_out"],
        "w1": a["L0_gnn_w1"],
        "b1_cols": columns(a["L0_gnn_b1"]),
        "w2": a["L0_gnn_w2"],
        "b2": a["L0_gnn_b2"],
        "ln_gamma": a["L0_gnn_ln_gamma"],
        "ln_beta": a["L0_gnn_ln_beta"],
        "wq_t": np.ascontiguousarray(a["L1_gnn_Wq"].T),
        "bq_cols": columns(a["L1_gnn_bq"]),
        "wk_t": np.ascontiguousarray(a["L1_gnn_Wk"].T),
        "bk_cols": columns(a["L1_gnn_bk"]),
        "wv_t": np.ascontiguousarray(a["L1_gnn_Wv"].T),
        "bv": a["L1_gnn_bv"],
        "wo_t": np.ascontiguousarray(a["L1_gnn_Wo"].T),
        "bo": a["L1_gnn_bo"],
        "identity": np.eye(128, dtype=np.float32),
    }
    nc = bacc.Bacc("TRN2", target_bir_lowering=False, num_devices=1)
    args = [nc.dram_tensor(k, v.shape, mb.dt.from_np(v.dtype), kind="ExternalInput").ap() for k, v in arrays.items()]
    out = nc.dram_tensor("out", (B, n, f), mb.dt.float32, kind="ExternalOutput").ap()
    gat_then_attention_kernel(nc, *args, out)
    r = run_bass_kernel_spmd(nc, [arrays], core_ids=[0])
    return r.results[0]["out"]
```
